# Optimizing a Trainium2 kernel written in Bass

```python
import numpy as np
import jax
import jax.numpy as jnp

def _softmax(x, axis=-1):
    return jax.nn.softmax(x, axis=axis)

def _gelu(x):
    return jax.nn.gelu(x, approximate=True)

def _silu(x):
    return jax.nn.silu(x)

def _sigmoid(x):
    return jax.nn.sigmoid(x)

def _layernorm(x, axis=-1, eps=1e-05):
    m = jnp.mean(x, axis=axis, keepdims=True)
    v = jnp.var(x, axis=axis, keepdims=True)
    return (x - m) / jnp.sqrt(v + eps)

def _scatter_add(tgt, idx, src, axis=0):
    return tgt.at[idx].add(src)

def _segment_sum(src, seg, n):
    return jax.ops.segment_sum(src, seg, n)
kernel_name = 'mk_adaln_d1_jaxref_r8_e9b776'

def setup_inputs(seed: int=0):
    np.random.seed(seed)
    _w = jnp.asarray

    def _L0_attn_setup():
        import jax, jax.numpy as jnp
        import numpy as np
        LANES = 4
        EPS = 1e-08

        def _rms_norm(z):
            return z * jax.lax.rsqrt(jnp.mean(z * z, axis=-1, keepdims=True) + EPS)

        def _combine(left, right, W):
            B, T, C = left.shape
            hd = C // LANES
            q = left.reshape(B, T, LANES, hd)
            k = right.reshape(B, T, LANES, hd)
            v = ((left + right) @ W).reshape(B, T, LANES, hd)
            scores = jnp.einsum('btld,btmd->btlm', q, k) * hd ** (-0.5)
            att = jax.nn.softmax(scores, axis=-1)
            z = jnp.einsum('btlm,btmd->btld', att, v)
            denom = (1.0 + jnp.arange(LANES, dtype=z.dtype))[None, None, :, None]
            z = _rms_norm(z) / denom
            return left + z.reshape(B, T, C)

        def _pscan2(x, W, identity):
            B, T, C = x.shape
            d = 1
            while d < T:
                ident = jnp.broadcast_to(identity.astype(x.dtype), (B, d, C))
                shifted = jnp.concatenate([ident, x[:, :-d]], axis=1)
                x = _combine(shifted, x, W)
                d *= 2
            return x

        def _reference_tuple_inner(x, W_up, W_v, W_proj, identity, W_scan_raw):
            U, _, Vt = jnp.linalg.svd(W_scan_raw, full_matrices=False)
            W = U @ Vt
            q = x @ W_up.T
            v = x @ W_v.T
            q = _pscan2(q, W, identity)
            Y = q * v @ W_proj.T
            return (Y, q)
        key = jax.random.key(seed)
        ks = jax.random.split(key, 6)
        B, T, C = (4, 256, 128)
        s = 0.02
        x = jax.random.normal(ks[0], (B, T, C), dtype=jnp.float32)
        W_up = jax.random.normal(ks[1], (C, C), dtype=jnp.float32) * s
        W_v = jax.random.normal(ks[2], (C, C), dtype=jnp.float32) * s
        W_proj = jax.random.normal(ks[3], (C, C), dtype=jnp.float32) * s
        identity = jax.random.uniform(ks[4], (C,), dtype=jnp.float32)
        W_scan_raw = jax.random.normal(ks[5], (C, C), dtype=jnp.float32) * s
        return {'x': x, 'W_up': W_up, 'W_v': W_v, 'W_proj': W_proj, 'identity': identity, 'W_scan_raw': W_scan_raw}
    _L0_attn_in = _L0_attn_setup()

    def _L0_ffn_setup():
        import jax, jax.numpy as jnp
        import numpy as np
        TOP_K = 2
        key = jax.random.key(seed)
        k0, k1, k2, k3 = jax.random.split(key, 4)
        B, T, C, E, F = (4, 256, 128, 8, 512)
        x = jax.random.normal(k0, (B, T, C), dtype=jnp.float32)
        gate_w = jax.random.normal(k1, (C, E), dtype=jnp.float32) * 0.02
        w1 = jax.random.normal(k2, (E, C, F), dtype=jnp.float32) * 0.02
        w2 = jax.random.normal(k3, (E, F, C), dtype=jnp.float32) * 0.02
        return {'x': x, 'gate_w': gate_w, 'w1': w1, 'w2': w2}
    _L0_ffn_in = _L0_ffn_setup()
    _L0_c = _w((lambda *s: np.random.randn(*s).astype(np.float32) * 0.05)(4, 128))
    _L0_wmod = _w((lambda *s: np.random.randn(*s).astype(np.float32) * 0.05)(128, 6 * 128) * 128 ** (-0.5))
    _d = {'L0_attn_x': _L0_attn_in['x'], 'L0_attn_W_up': _L0_attn_in['W_up'], 'L0_attn_W_v': _L0_attn_in['W_v'], 'L0_attn_W_proj': _L0_attn_in['W_proj'], 'L0_attn_identity': _L0_attn_in['identity'], 'L0_attn_W_scan_raw': _L0_attn_in['W_scan_raw'], 'L0_ffn_gate_w': _L0_ffn_in['gate_w'], 'L0_ffn_w1': _L0_ffn_in['w1'], 'L0_ffn_w2': _L0_ffn_in['w2'], 'L0_c': _L0_c, 'L0_wmod': _L0_wmod}
    _x0 = _d['L0_attn_x']
    _d['L0_attn_x'] = jax.random.normal(jax.random.fold_in(jax.random.key(seed), 1), (4, 1024, 128), dtype=_x0.dtype)
    del _x0
    return _d

def reference(L0_attn_x, L0_attn_W_up, L0_attn_W_v, L0_attn_W_proj, L0_attn_identity, L0_attn_W_scan_raw, L0_ffn_gate_w, L0_ffn_w1, L0_ffn_w2, L0_c, L0_wmod):

    def _L0_attn_ref(x, W_up, W_v, W_proj, identity, W_scan_raw):
        import jax, jax.numpy as jnp
        import numpy as np
        LANES = 4
        EPS = 1e-08

        def _rms_norm(z):
            return z * jax.lax.rsqrt(jnp.mean(z * z, axis=-1, keepdims=True) + EPS)

        def _combine(left, right, W):
            B, T, C = left.shape
            hd = C // LANES
            q = left.reshape(B, T, LANES, hd)
            k = right.reshape(B, T, LANES, hd)
            v = ((left + right) @ W).reshape(B, T, LANES, hd)
            scores = jnp.einsum('btld,btmd->btlm', q, k) * hd ** (-0.5)
            att = jax.nn.softmax(scores, axis=-1)
            z = jnp.einsum('btlm,btmd->btld', att, v)
            denom = (1.0 + jnp.arange(LANES, dtype=z.dtype))[None, None, :, None]
            z = _rms_norm(z) / denom
            return left + z.reshape(B, T, C)

        def _pscan2(x, W, identity):
            B, T, C = x.shape
            d = 1
            while d < T:
                ident = jnp.broadcast_to(identity.astype(x.dtype), (B, d, C))
                shifted = jnp.concatenate([ident, x[:, :-d]], axis=1)
                x = _combine(shifted, x, W)
                d *= 2
            return x

        def _reference_tuple_inner(x, W_up, W_v, W_proj, identity, W_scan_raw):
            U, _, Vt = jnp.linalg.svd(W_scan_raw, full_matrices=False)
            W = U @ Vt
            q = x @ W_up.T
            v = x @ W_v.T
            q = _pscan2(q, W, identity)
            Y = q * v @ W_proj.T
            return (Y, q)
        return _reference_tuple_inner(x, W_up, W_v, W_proj, identity, W_scan_raw)[0]

    def _L0_ffn_ref(x, gate_w, w1, w2):
        import jax, jax.numpy as jnp
        import numpy as np
        TOP_K = 2
        E = gate_w.shape[-1]
        probs = jax.nn.softmax(x @ gate_w, axis=-1)
        topw, topi = jax.lax.top_k(probs, TOP_K)
        topw = topw / topw.sum(axis=-1, keepdims=True)
        combine = (jax.nn.one_hot(topi, E, dtype=x.dtype) * topw[..., None]).sum(axis=-2)

        def body(acc, params):
            w1_i, w2_i, cw = params
            h = jax.nn.gelu(x @ w1_i, approximate=False)
            return (acc + cw[..., None] * (h @ w2_i), None)
        acc0 = jnp.zeros_like(x)
        out, _ = jax.lax.scan(body, acc0, (w1, w2, jnp.moveaxis(combine, -1, 0)))
        return out
    x = L0_attn_x
    mod = (_silu(L0_c) @ L0_wmod).reshape(L0_c.shape[0], 6, 1, -1)
    sa, ca, ga, sb, cb, gb = (mod[:, 0], mod[:, 1], mod[:, 2], mod[:, 3], mod[:, 4], mod[:, 5])
    ga = (2 * (ga >= 0) - 1) * jnp.maximum(jnp.abs(ga), 0.25)
    gb = (2 * (gb >= 0) - 1) * jnp.maximum(jnp.abs(gb), 0.25)
    h = _layernorm(x, axis=-1) * (1 + ca) + sa
    x = x + ga * _L0_attn_ref(h, L0_attn_W_up, L0_attn_W_v, L0_attn_W_proj, L0_attn_identity, L0_attn_W_scan_raw)
    h = _layernorm(x, axis=-1) * (1 + cb) + sb
    x = x + gb * _L0_ffn_ref(h, L0_ffn_gate_w, L0_ffn_w1, L0_ffn_w2)
    return x

_drawn_inputs = setup_inputs


def setup_inputs(seed=0):
    import zlib

    import numpy as np

    out = dict(_drawn_inputs(seed))
    spreads = {}
    factors = {'L0_attn_W_up': 6.227,
     'L0_attn_W_v': 4.45,
     'L0_attn_W_proj': 4.441,
     'L0_attn_identity': 7.722,
     'L0_attn_W_scan_raw': 4.659,
     'L0_ffn_gate_w': 6.8,
     'L0_ffn_w1': 6.068,
     'L0_ffn_w2': 5.967,
     'L0_c': 3.531,
     'L0_wmod': 3.665}
    for name, (base, spread) in spreads.items():
        noise = np.random.default_rng([zlib.crc32(name.encode()), seed]).standard_normal(out[name].shape)
        drawn = base * np.exp(spread * noise) if base else spread * noise
        out[name] = jnp.asarray(drawn.astype(out[name].dtype))
    for name, factor in factors.items():
        out[name] = (out[name] * factor).astype(out[name].dtype)
    return out
```

```python
from contextlib import ExitStack

import concourse.bass as bass
from concourse import mybir

F32 = mybir.dt.float32
ALU = mybir.AluOpType
ACT = mybir.ActivationFunctionType
AX = mybir.AxisListType.X

P = 128
LANES = 4
GROW, GROW_STEPS = (3.4445, -4.7750, 2.0315), 11
POLISH, POLISH_STEPS = (1.875, -1.25, 0.375), 3


def adaln_block(nc, x, W_up, W_v, W_proj, identity, W_scan_raw, gate_w, w1, w2, c, wmod, out):
    B, T, C = x.shape
    E, _, F = w1.shape
    J = T // P
    HD = C // LANES
    KEYS = LANES - 1
    FC = F // P
    SCALE = float(HD) ** -0.5
    LEVELS = T.bit_length() - 1
    SPLIT = 2
    assert C == P and J == 8

    order = [(b, n) for pair in range(0, B, 2) for n in range(LEVELS) for b in (pair, pair + 1)]
    SA, CA, GA, SB, CB, GB = range(6)

    with ExitStack() as ctx:
        def sb(name, shape, dt=F32):
            return ctx.enter_context(nc.sbuf_tensor(name, shape, dt))

        def ps(name, shape):
            return ctx.enter_context(nc.psum_tensor(name, shape, F32))

        def sem(name):
            return ctx.enter_context(nc.semaphore(name))

        eye = sb("eye", [P, P])
        eye_grow = sb("eye_grow", [P, P])
        eye_polish = sb("eye_polish", [P, P])
        ones = sb("ones", [P, P])
        w_t = sb("w_t", [P, 3, P])
        scan_raw = sb("scan_raw", [P, P])
        w_scan = sb("w_scan", [P, P])
        gate = sb("gate", [P, E])
        w1_sb = sb("w1_sb", [P, E, F])
        w2_sb = sb("w2_sb", [P, E, FC, C])
        ct = sb("ct", [P, B])
        ct_e = sb("ct_e", [P, B])
        ct_silu = sb("ct_silu", [P, B])
        mod = sb("mod", [P, B, 6, C])
        ident_row = sb("ident_row", [P // 2, C])
        ident = sb("ident", [P // 2, J, C])
        lane_sq = sb("lane_sq", [P, J, LANES])
        before = sb("before", [P, E, E])

        gram = sb("gram", [P, P])
        gram_sq = sb("gram_sq", [P, P])
        gram_t = sb("gram_t", [P, P])
        poly = sb("poly", [P, P])
        polar = sb("polar", [P, 2, P])
        norm_in = sb("norm_in", [P, 1])
        norm_ln = sb("norm_ln", [P, 1])
        norm = sb("norm", [P, 1])

        x_sb = sb("x_sb", [P, B, J, C])
        q_sb = sb("q_sb", [P, B, J, C])
        v_sb = sb("v_sb", [P, B, J, C])

        left = sb("left", [P, 2, J, C])
        both = sb("both", [P, 2, J, C])
        both_t = sb("both_t", [P, J * P])
        keys = sb("keys", [P, 2, J, KEYS, HD])
        prod = sb("prod", [P, 2, J, LANES, KEYS, HD])
        early = prod[:].rearrange("p s j l m d -> p (s j l m d)")
        wmod_sb = early[:, 0:6 * C]
        w_raw = early[:, 6 * C:6 * C + 3 * P].rearrange("p (n c) -> p n c", n=3)
        score = sb("score", [P, 2, J, LANES, KEYS])
        low = sb("low", [P, 2, J, LANES])
        shifted = sb("shifted", [P, 2, J, LANES, LANES])
        expo = sb("expo", [P, 2, J, LANES, LANES])
        total = sb("total", [P, 2, J, LANES])
        recip = sb("recip", [P, 2, J, LANES])
        att = sb("att", [P, 2, J, LANES, KEYS])
        z = sb("z", [P, 2, J, C])
        z_sq = both
        ms = sb("ms", [P, 2, J, LANES])
        arg = sb("arg", [P, 2, J, LANES])
        ln_arg = sb("ln_arg", [P, 2, J, LANES])
        guess = sb("guess", [P, 2, J, LANES])
        newton = sb("newton", [P, 2, J, LANES])
        root = sb("root", [P, 2, J, LANES])

        centred = sb("centred", [P, J, C])
        sign, size = centred[:, 0:B], centred[:, B:2 * B]
        h_sb = sb("h_sb", [P, J, C])
        h_t = sb("h_t", [P, J * P])
        stat = sb("stat", [P, 8, J])
        h2_t = sb("h2_t", [P, 2, J * P])
        logit = sb("logit", [P, J, E])
        beat = centred[:, 0:J // 2].rearrange("p j (a i k) -> p (j a) i k", i=E, k=E)
        tie = centred[:, J // 2:J].rearrange("p j (a i k) -> p (j a) i k", i=E, k=E)
        rank = sb("rank", [P, J, E])
        route_e = sb("route_e", [P, J, E])
        route_s = sb("route_s", [P, 3, J])
        weight = sb("weight", [P, 2, J, E])
        hidden = sb("hidden", [P, 2, FC, 512])
        acc = centred

        ps_t = ps("ps_t", [P, J * P])
        ps_v = ps("ps_v", [P, J * P])
        ps_h = ps("ps_h", [P, 2, 512])
        ps_y = ps("ps_y", [P, 2, 512])

        weights_in, polar_in, mod_in, x_in, ident_in, experts_in = (
            sem(n) for n in ("weights_in", "polar_in", "mod_in", "x_in", "ident_in", "experts_in"))
        consts = sem("consts")
        dve_const = sem("dve_const")
        ident_ready = sem("ident_ready")
        wt_done, wt_copied = sem("wt_done"), sem("wt_copied")
        silu_exp, silu_ready = sem("silu_exp"), sem("silu_ready")
        mod_done, mod_copied, mod_ready = sem("mod_done"), sem("mod_copied"), sem("mod_ready")
        gram_done, gram_copied, gram_t_ready = sem("gram_done"), sem("gram_copied"), sem("gram_t_ready")
        square_done, poly_ready = sem("square_done"), sem("poly_ready")
        next_done, next_copied, next_t_copied = sem("next_done"), sem("next_copied"), sem("next_t_copied")
        norm_sum, norm_total, norm_ready, w_scan_ready = (
            sem("norm_sum"), sem("norm_total"), sem("norm_ready"), sem("w_scan_ready"))
        t_full, t_free, v_full, v_free = sem("t_full"), sem("t_free"), sem("v_full"), sem("v_free")
        h_full, h_free, y_full, y_free = sem("h_full"), sem("h_free"), sem("y_full"), sem("y_free")
        centred_ready, sq_ready, var_ready, var_exp, h_ready = (
            sem("centred_ready"), sem("sq_ready"), sem("var_ready"), sem("var_exp"), sem("h_ready"))
        left_in = [sem("left_in0"), sem("left_in1")]
        keys_ready, both_ready, pool_prod = sem("keys_ready"), sem("both_ready"), sem("pool_prod")
        shifted_ready, expo_ready, z_ready, zsq_ready = (
            sem("shifted_ready"), sem("expo_ready"), sem("z_ready"), sem("zsq_ready"))
        arg_ready, guess_ready, scaled_ready, state_ready = (
            sem("arg_ready"), sem("guess_ready"), sem("scaled_ready"), sem("state_ready"))
        qv_ready, route_exp = (
            sem("qv_ready"), sem("route_exp"))
        hidden_ready, final_ready, stored = sem("hidden_ready"), sem("final_ready"), sem("stored")
        dve_done, act_done, pool_done = sem("dve_done"), sem("act_done"), sem("pool_done")

        t_use, v_use = {}, {}
        for b in range(B):
            t_use["h", b] = len(t_use)
            v_use["q", b], v_use["v", b] = len(v_use), len(v_use) + 1
        for s in order:
            t_use[s], v_use[s] = len(t_use), len(v_use)
        for b in range(B):
            t_use["qv", b], t_use["h2", b] = len(t_use), len(t_use) + 1
            v_use["proj", b], v_use["gate", b] = len(v_use), len(v_use) + 1

        def steps(shape_of):
            return [shape_of[:, j * P:(j + 1) * P] for j in range(J)]

        def left_dmas(level):
            return 3 if (1 << level) < J else 2

        def left_count(b, level):
            earlier = [n for (bb, n) in order[:order.index((b, level)) + 1] if bb % 2 == b % 2]
            return 16 * sum(left_dmas(n) for n in earlier)

        block = ctx.enter_context(nc.Block())

        @block.sync
        def _(sp):
            sp.dma_start(scan_raw[:], W_scan_raw).then_inc(polar_in, 16)
            sp.dma_start(wmod_sb, wmod).then_inc(mod_in, 16)
            for b in range(B):
                sp.dma_start(x_sb[:, b], x[b].rearrange("(p j) c -> p j c", j=J)).then_inc(x_in, 16)
            sp.dma_start(w1_sb[:], w1.rearrange("e c f -> c e f")).then_inc(experts_in, 16)
            sp.dma_start(w2_sb[:], w2.rearrange("e (k p) c -> p e k c", p=P)).then_inc(experts_in, 16)

            sp.wait_ge(ident_ready, 1)
            for n, (b, level) in enumerate(order):
                d = 1 << level
                if level == 0:
                    sp.wait_ge(v_free, v_use["q", b] + 1)
                    if b >= 2:
                        sp.wait_ge(state_ready, order.index((b - 2, LEVELS - 1)) + 1)
                else:
                    sp.wait_ge(state_ready, order.index((b, level - 1)) + 1)
                dst, src = left[:, b % 2], q_sb[:, b]
                if d < J:
                    sp.dma_start(dst[:, d:J], src[:, 0:J - d]).then_inc(left_in[b % 2], 16)
                    sp.dma_start(dst[1:P, 0:d], src[0:P - 1, J - d:J]).then_inc(left_in[b % 2], 16)
                    sp.dma_start(dst[0:1, 0:d], ident[0:1, 0:d]).then_inc(left_in[b % 2], 16)
                else:
                    a = d // J
                    sp.dma_start(dst[a:P], src[0:P - a]).then_inc(left_in[b % 2], 16)
                    sp.dma_start(dst[0:a], ident[0:a]).then_inc(left_in[b % 2], 16)

            for b in range(B):
                sp.wait_ge(final_ready, b + 1)
                sp.dma_start(out[b].rearrange("(p j) c -> p j c", j=J), x_sb[:, b]).then_inc(stored, 16)
            sp.wait_ge(stored, 16 * B)

        @block.gpsimd
        def _(pool):
            nc.gpsimd.memset(eye[:], 0.0).then_inc(pool_done, 1)
            nc.gpsimd.memset(before[:], 0.0).then_inc(pool_done, 1)
            pool.wait_ge(pool_done, 2)
            nc.gpsimd.affine_select(out=eye[:], in_=eye[:], compare_op=ALU.not_equal, fill=1.0, base=0,
                                    pattern=[[-1, P]], channel_multiplier=1).then_inc(consts, 1)
            nc.gpsimd.affine_select(out=before[:], in_=before[:], compare_op=ALU.is_ge, fill=1.0, base=0,
                                    pattern=[[-1, E], [1, E]], channel_multiplier=0).then_inc(consts, 1)
            pool.wait_ge(ident_in, 16)
            nc.gpsimd.tensor_copy(ident[:], ident_row[:].rearrange("p (j c) -> p j c", j=1)
                                  .to_broadcast([P // 2, J, C])).then_inc(ident_ready, 1)
            count = 2

            def start(n):
                b, level = order[n]
                s = b % 2
                q4 = q_sb[:, b].rearrange("p j (l d) -> p j l d", l=LANES)
                if level == 0:
                    pool.wait_ge(v_free, v_use["q", b] + 1)
                else:
                    pool.wait_ge(state_ready, order.index((b, level - 1)) + 1)
                if n >= 2:
                    pool.wait_ge(z_ready, n - 1)
                k0 = q4[:, :, 0:1, :].to_broadcast([P, J, KEYS, HD])
                nc.gpsimd.tensor_tensor(keys[:, s], q4[:, :, 1:LANES, :], k0, ALU.subtract).then_inc(keys_ready, 1)
                pool.wait_ge(left_in[s], left_count(b, level))
                nc.gpsimd.tensor_tensor(both[:, s], q_sb[:, b], left[:, s], ALU.add).then_inc(both_ready, 1)
                pool.wait_ge(keys_ready, n + 1)
                l4 = left[:, s].rearrange("p j (l d) -> p j l d", l=LANES)
                for l in range(SPLIT, LANES):
                    last = nc.gpsimd.tensor_tensor(
                        prod[:, s, :, l], l4[:, :, l:l + 1, :].to_broadcast([P, J, KEYS, HD]), keys[:, s], ALU.mult)
                last.then_inc(pool_prod, 1)

            def finish(n):
                b, level = order[n]
                s = b % 2
                pool.wait_ge(scaled_ready, n + 1)
                nc.gpsimd.tensor_tensor(q_sb[:, b], left[:, s], z[:, s], ALU.add).then_inc(state_ready, 1)

            for n in range(len(order)):
                start(n)
                if n >= 1:
                    finish(n - 1)
            finish(len(order) - 1)

        @block.scalar
        def _(act):
            act.dma_start(ct[:], c.rearrange("b c -> c b"), allow_slow_non_contiguous=True).then_inc(mod_in, 16)
            act.dma_start(w_raw[:, 0], W_up).then_inc(weights_in, 16)
            act.dma_start(w_raw[:, 1], W_v).then_inc(weights_in, 16)
            act.dma_start(w_raw[:, 2], W_proj).then_inc(weights_in, 16)
            act.dma_start(gate[:], gate_w).then_inc(weights_in, 16)
            act.dma_start(ident_row[:], identity.rearrange("(a c) -> a c", a=1)
                          .to_broadcast([P // 2, C])).then_inc(ident_in, 16)
            nc.scalar.preload_act_table_set("natural_log_exp_and_others")
            act.wait_ge(mod_in, 32)
            nc.scalar.activation(ct_e[:], ct[:], ACT.Exp, scale=-1.0).then_inc(silu_exp, 1)
            for b in range(B):
                act.wait_ge(mod_done, b + 1)
                nc.scalar.activation(mod[:, b].rearrange("p (a m) c -> p a (m c)", a=2), ps_h[:, :, 0:3 * C],
                                     ACT.Copy).then_inc(mod_copied, 1)
            act.wait_ge(wt_done, 1)
            nc.scalar.activation(w_t[:], ps_y[:, 0, 0:3 * P].rearrange("p (n c) -> p n c", n=3),
                                 ACT.Copy).then_inc(wt_copied, 1)

            act.wait_ge(gram_done, 1)
            nc.scalar.activation(gram_sq[:], ps_h[:, 0, 0:P], ACT.Square, accum_out=norm_in[:]).then_inc(norm_sum, 1)
            act.wait_ge(norm_total, 2)
            nc.scalar.activation(norm_ln[:], norm_in[:], ACT.Ln).then_inc(act_done, 1)
            act.wait_ge(act_done, 1)
            nc.scalar.activation(norm[:], norm_ln[:], ACT.Exp, scale=-0.25).then_inc(norm_ready, 1)
            act.wait_ge(norm_ready, 1)
            nc.scalar.activation(polar[:, 0], scan_raw[:], ACT.Copy, scale=norm[:]).then_inc(next_copied, 1)
            act.wait_ge(gram_done, 2)
            nc.scalar.activation(polar[:, 1], ps_h[:, 0, P:2 * P], ACT.Copy, scale=norm[:]).then_inc(next_t_copied, 1)
            for k in range(GROW_STEPS + POLISH_STEPS):
                act.wait_ge(next_done, k + 1)
                nc.scalar.activation(polar[:, 1], ps_y[:, 1, 0:P], ACT.Copy).then_inc(next_t_copied, 1)

            def evacuate(dst, key):
                act.wait_ge(t_full, t_use[key] + 1)
                nc.scalar.activation(dst, ps_t[:], ACT.Copy).then_inc(t_free, 1)

            def inverse_root(k):
                act.wait_ge(centred_ready, k + 1)
                nc.scalar.activation(h_sb[:], centred[:], ACT.Square, scale=float(C) ** -0.5).then_inc(sq_ready, 1)
                act.wait_ge(var_ready, k + 1)
                nc.scalar.activation(stat[:, 2], stat[:, 1], ACT.Ln).then_inc(sq_ready, 1)
                act.wait_ge(sq_ready, 2 * k + 2)
                nc.scalar.activation(stat[:, 3], stat[:, 2], ACT.Exp, scale=-0.5).then_inc(var_exp, 1)

            for b in range(B):
                inverse_root(b)
                if b >= 1:
                    act.wait_ge(v_full, v_use["v", b - 1] + 1)
                evacuate(h_t[:], ("h", b))
                act.wait_ge(v_full, v_use["q", b] + 1)
                nc.scalar.activation(q_sb[:, b].rearrange("p j c -> p (j c)"), ps_v[:], ACT.Copy).then_inc(v_free, 1)
                act.wait_ge(v_full, v_use["v", b] + 1)
                nc.scalar.activation(v_sb[:, b].rearrange("p j c -> p (j c)"), ps_v[:], ACT.Copy).then_inc(v_free, 1)

            def root_guess(n):
                s = order[n][0] % 2
                act.wait_ge(arg_ready, n + 1)
                nc.scalar.activation(ln_arg[:, s], arg[:, s], ACT.Ln).then_inc(act_done, 1)
                act.wait_ge(act_done, n + 2)
                nc.scalar.activation(guess[:, s], ln_arg[:, s], ACT.Exp, scale=-0.5).then_inc(guess_ready, 1)

            for n, (b, level) in enumerate(order):
                s = b % 2
                if n >= 1:
                    act.wait_ge(v_full, v_use[order[n - 1]] + 1)
                evacuate(both_t[:], (b, level))
                if n >= 1:
                    root_guess(n - 1)
                act.wait_ge(shifted_ready, n + 1)
                nc.scalar.activation(expo[:, s], shifted[:, s], ACT.Exp, scale=SCALE).then_inc(expo_ready, 1)
                act.wait_ge(z_ready, n + 1)
                nc.scalar.activation(z_sq[:, s], z[:, s], ACT.Square, scale=float(HD) ** -0.5).then_inc(zsq_ready, 1)
            root_guess(len(order) - 1)

            for b in range(B):
                evacuate(h_t[:], ("qv", b))
                inverse_root(B + b)
                evacuate(h2_t[:, b % 2], ("h2", b))
                act.wait_ge(v_free, v_use["gate", b] + 1)
                nc.scalar.activation(route_e[:], logit[:], ACT.Exp).then_inc(route_exp, 1)
                for half in range(2):
                    for e in range(E):
                        g = (b * 2 + half) * E + e
                        if g >= 2:
                            act.wait_ge(y_full, g - 1)
                        for f in range(FC):
                            act.wait_ge(h_full, g * FC + f + 1)
                            nc.scalar.activation(hidden[:, g % 2, f], ps_h[:, f % 2], ACT.Gelu).then_inc(h_free, 1)

        @block.tensor
        def _(pe):
            pe.wait_ge(silu_ready, 1)
            for b in range(B):
                if b >= 1:
                    pe.wait_ge(mod_copied, b)
                for a in range(2):
                    last = nc.tensor.matmul(ps_h[:, a, 0:3 * C], ct_silu[:, b:b + 1].to_broadcast([P, P]),
                                            wmod_sb[:, a * 3 * C:(a + 1) * 3 * C], start=True, stop=True)
                last.then_inc(mod_done, 1)
            pe.wait_ge(consts, 2)
            pe.wait_ge(weights_in, 64)
            for n in range(3):
                last = nc.tensor.transpose(ps_y[:, 0, n * P:(n + 1) * P], w_raw[:, n], eye[:])
            last.then_inc(wt_done, 1)

            pe.wait_ge(mod_copied, B)
            pe.wait_ge(polar_in, 16)
            nc.tensor.matmul(ps_h[:, 0, 0:P], scan_raw[:], scan_raw[:], start=True, stop=True).then_inc(gram_done, 1)
            pe.wait_ge(norm_sum, 1)
            pe.wait_ge(dve_const, 3)
            nc.tensor.matmul(ps_h[:, 1, 0:1], ones[:], norm_in[:], start=True, stop=True).then_inc(norm_total, 1)
            nc.tensor.transpose(ps_h[:, 0, P:2 * P], scan_raw[:], eye[:]).then_inc(gram_done, 1)
            for k in range(GROW_STEPS + POLISH_STEPS):
                pe.wait_ge(next_copied, k + 1)
                pe.wait_ge(next_t_copied, k + 1)
                nc.tensor.matmul(ps_h[:, 0, 0:P], polar[:, 0], polar[:, 0], start=True, stop=True).then_inc(gram_done, 1)
                pe.wait_ge(gram_copied, k + 1)
                nc.tensor.matmul(ps_h[:, 1, 0:P], gram[:], gram[:], start=True, stop=True).then_inc(square_done, 1)
                pe.wait_ge(poly_ready, k + 1)
                if k == 0:
                    pe.wait_ge(wt_copied, 1)
                nc.tensor.matmul(ps_y[:, 0, 0:P], polar[:, 1], poly[:], start=True, stop=True)
                nc.tensor.matmul(ps_y[:, 1, 0:P], poly[:], polar[:, 1], start=True, stop=True).then_inc(next_done, 1)

            def transposes(src, key):
                if t_use[key] >= 1:
                    pe.wait_ge(t_free, t_use[key])
                for j in range(J):
                    last = nc.tensor.transpose(ps_t[:, j * P:(j + 1) * P], src[:, j], eye[:])
                last.then_inc(t_full, 1)

            def products(src_t, rhs, key, width):
                if v_use[key] >= 1:
                    pe.wait_ge(v_free, v_use[key])
                for j in range(J):
                    last = nc.tensor.matmul(ps_v[:, j * width:(j + 1) * width], src_t[:, j * P:(j + 1) * P], rhs,
                                            start=True, stop=True)
                last.then_inc(v_full, 1)

            for b in range(B):
                pe.wait_ge(h_ready, b + 1)
                transposes(h_sb, ("h", b))
                pe.wait_ge(t_free, t_use["h", b] + 1)
                products(h_t, w_t[:, 0], ("q", b), C)
                products(h_t, w_t[:, 1], ("v", b), C)

            pe.wait_ge(w_scan_ready, 1)
            for n, (b, level) in enumerate(order):
                pe.wait_ge(both_ready, n + 1)
                transposes(both[:, b % 2], (b, level))
                pe.wait_ge(t_free, t_use[b, level] + 1)
                products(both_t, w_scan[:], (b, level), C)

            for b in range(B):
                pe.wait_ge(qv_ready, b + 1)
                transposes(h_sb, ("qv", b))
                pe.wait_ge(t_free, t_use["qv", b] + 1)
                products(h_t, w_t[:, 2], ("proj", b), C)
                pe.wait_ge(h_ready, B + b + 1)
                transposes(h_sb, ("h2", b))
                pe.wait_ge(t_free, t_use["h2", b] + 1)
                products(h2_t[:, b % 2], gate[:], ("gate", b), E)
                if b == 0:
                    pe.wait_ge(experts_in, 32)

                def up(g):
                    half, e = g // E % 2, g % E
                    for f in range(FC):
                        k = g * FC + f
                        if k >= 2:
                            pe.wait_ge(h_free, k - 1)
                        nc.tensor.matmul(ps_h[:, f % 2], w1_sb[:, e, f * P:(f + 1) * P],
                                         h2_t[:, b % 2, half * 512:(half + 1) * 512],
                                         start=True, stop=True).then_inc(h_full, 1)

                def down(g):
                    e = g % E
                    pe.wait_ge(h_free, (g + 1) * FC)
                    if g >= 2:
                        pe.wait_ge(y_free, g - 1)
                    for jj in range(4):
                        for f in range(FC):
                            last = nc.tensor.matmul(ps_y[:, g % 2, jj * P:(jj + 1) * P],
                                                    hidden[:, g % 2, f, jj * P:(jj + 1) * P], w2_sb[:, e, f],
                                                    start=(f == 0), stop=(f == FC - 1))
                    last.then_inc(y_full, 1)

                for g in range(b * 2 * E, (b + 1) * 2 * E):
                    up(g)
                    if g > b * 2 * E:
                        down(g - 1)
                down((b + 1) * 2 * E - 1)

        @block.vector
        def _(dve):
            count = [0]

            def step(ins):
                ins.then_inc(dve_done, 1)
                count[0] += 1
                return count[0]

            def after(n):
                dve.wait_ge(dve_done, n)

            tt, ts, stt = nc.vector.tensor_tensor, nc.vector.tensor_scalar, nc.vector.scalar_tensor_tensor
            nc.vector.memset(ones[:], 1.0).then_inc(dve_const, 1)
            for l in range(LANES):
                last = nc.vector.memset(lane_sq[:, :, l:l + 1], float((l + 1) ** 2))
            last.then_inc(dve_const, 1)
            dve.wait_ge(consts, 1)
            after(step(ts(eye_grow[:], eye[:], GROW[0], None, ALU.mult)))
            ts(eye_polish[:], eye[:], POLISH[0], None, ALU.mult).then_inc(dve_const, 1)

            dve.wait_ge(silu_exp, 1)
            k = step(ts(ct_e[:], ct_e[:], 1.0, None, ALU.add))
            after(k)
            k = step(nc.vector.reciprocal(ct_e[:], ct_e[:]))
            after(k)
            tt(ct_silu[:], ct[:], ct_e[:], ALU.mult).then_inc(silu_ready, 1)

            dve.wait_ge(mod_copied, B)
            for m in (CA, CB):
                step(ts(mod[:, :, m], mod[:, :, m], 1.0, None, ALU.add))
            for m in (GA, GB):
                step(ts(sign, mod[:, :, m], 0.0, 2.0, ALU.is_ge, ALU.mult))
                k = step(stt(out=size, in0=mod[:, :, m], scalar=-1.0, in1=mod[:, :, m], op0=ALU.mult, op1=ALU.max))
                after(k)
                k = step(ts(size, size, 0.25, None, ALU.max))
                after(k)
                k = step(stt(out=mod[:, :, m], in0=sign, scalar=-1.0, in1=size, op0=ALU.add, op1=ALU.mult))
                after(k)

            dve.wait_ge(dve_const, 3)
            dve.wait_ge(norm_total, 1)
            ts(norm_in[:], ps_h[:, 1, 0:1], 1e-18, None, ALU.max).then_inc(norm_total, 1)
            for k in range(GROW_STEPS + POLISH_STEPS):
                grow = k < GROW_STEPS
                (_, cb, cc), eye_a = (GROW, eye_grow) if grow else (POLISH, eye_polish)
                dve.wait_ge(gram_done, k + 3)
                nc.vector.tensor_copy(gram[:], ps_h[:, 0, 0:P]).then_inc(gram_copied, 1)
                stt(out=gram_t[:], in0=ps_h[:, 0, 0:P], scalar=cb, in1=eye_a[:], op0=ALU.mult,
                    op1=ALU.add).then_inc(gram_t_ready, 1)
                dve.wait_ge(square_done, k + 1)
                dve.wait_ge(gram_t_ready, k + 1)
                stt(out=poly[:], in0=ps_h[:, 1, 0:P], scalar=cc, in1=gram_t[:], op0=ALU.mult,
                    op1=ALU.add).then_inc(poly_ready, 1)
                dve.wait_ge(next_done, k + 1)
                nc.vector.tensor_copy(polar[:, 0], ps_y[:, 0, 0:P]).then_inc(next_copied, 1)
            dve.wait_ge(next_copied, GROW_STEPS + POLISH_STEPS + 1)
            nc.vector.tensor_copy(w_scan[:, 0:HD], polar[:, 0, 0:HD])
            tt(w_scan[:, HD:].rearrange("p (m d) -> p m d", d=HD), polar[:, 0, HD:].rearrange("p (m d) -> p m d", d=HD),
               polar[:, 0, 0:HD].rearrange("p (m d) -> p m d", m=1).to_broadcast([P, KEYS, HD]),
               ALU.subtract).then_inc(w_scan_ready, 1)

            def rows(b, m):
                return mod[:, b, m:m + 1, :].to_broadcast([P, J, C])

            def per_token(a):
                return a.rearrange("p (j c) -> p j c", c=1).to_broadcast([P, J, C])

            def layernorm(k, b, scale_row, shift_row):
                n = step(nc.vector.tensor_reduce(stat[:, 0], x_sb[:, b], AX, ALU.add))
                after(n)
                stt(out=centred[:], in0=per_token(stat[:, 0]), scalar=-1.0 / C, in1=x_sb[:, b], op0=ALU.mult,
                    op1=ALU.add).then_inc(centred_ready, 1)
                dve.wait_ge(sq_ready, 2 * k + 1)
                n = step(nc.vector.tensor_reduce(stat[:, 4], h_sb[:], AX, ALU.add))
                after(n)
                ts(stat[:, 1], stat[:, 4], 1e-5, None, ALU.add).then_inc(var_ready, 1)
                dve.wait_ge(var_exp, k + 1)
                n = step(tt(stat[:, 5], stat[:, 3], stat[:, 3], ALU.mult))
                after(n)
                n = step(stt(out=stat[:, 6], in0=stat[:, 5], scalar=-0.5, in1=stat[:, 1], op0=ALU.mult, op1=ALU.mult))
                after(n)
                n = step(stt(out=stat[:, 7], in0=stat[:, 6], scalar=1.5, in1=stat[:, 3], op0=ALU.add, op1=ALU.mult))
                after(n)
                n = step(tt(centred[:], centred[:], per_token(stat[:, 7]), ALU.mult))
                after(n)
                n = step(tt(centred[:], centred[:], rows(b, scale_row), ALU.mult))
                after(n)
                tt(h_sb[:], centred[:], rows(b, shift_row), ALU.add).then_inc(h_ready, 1)

            for b in range(B):
                dve.wait_ge(x_in, 16 * B)
                if b >= 1:
                    dve.wait_ge(t_full, t_use["h", b - 1] + 1)
                layernorm(b, b, CA, SA)

            def scores(n):
                b, level = order[n]
                s = b % 2
                dve.wait_ge(keys_ready, n + 1)
                dve.wait_ge(left_in[s], left_count(b, level))
                l4 = left[:, s].rearrange("p j (l d) -> p j l d", l=LANES)
                for l in range(SPLIT):
                    last = tt(prod[:, s, :, l], l4[:, :, l:l + 1, :].to_broadcast([P, J, KEYS, HD]), keys[:, s], ALU.mult)
                return step(last)

            def soften(n, made):
                s = order[n][0] % 2
                after(made)
                step(nc.vector.tensor_reduce(score[:, s, :, 0:SPLIT], prod[:, s, :, 0:SPLIT], AX, ALU.add))
                dve.wait_ge(pool_prod, n + 1)
                k = step(nc.vector.tensor_reduce(score[:, s, :, SPLIT:], prod[:, s, :, SPLIT:], AX, ALU.add))
                after(k)
                k = step(nc.vector.tensor_reduce(low[:, s], score[:, s], AX, ALU.max, negate=True))
                after(k)
                k = step(ts(shifted[:, s, :, :, 0], low[:, s], 0.0, None, ALU.min))
                after(k)
                tt(shifted[:, s, :, :, 1:], score[:, s], shifted[:, s, :, :, 0:1].to_broadcast([P, J, LANES, KEYS]),
                   ALU.add).then_inc(shifted_ready, 1)

            def mix(n):
                b, level = order[n]
                s = b % 2
                dve.wait_ge(expo_ready, n + 1)
                k = step(nc.vector.tensor_reduce(total[:, s], expo[:, s], AX, ALU.add))
                after(k)
                k = step(nc.vector.reciprocal(recip[:, s], total[:, s]))
                after(k)
                k = step(tt(att[:, s], expo[:, s, :, :, 1:], recip[:, s].rearrange("p j (l m) -> p j l m", m=1)
                            .to_broadcast([P, J, LANES, KEYS]), ALU.mult))
                after(k)
                dve.wait_ge(v_full, v_use[b, level] + 1)
                v4 = ps_v[:].rearrange("p (j m d) -> p j m d", m=LANES, d=HD)
                for l in range(LANES):
                    k = step(tt(prod[:, s, :, l], att[:, s, :, l].rearrange("p j (m d) -> p j m d", d=1)
                                .to_broadcast([P, J, KEYS, HD]), v4[:, :, 1:], ALU.mult))
                after(k)
                z4 = z[:, s].rearrange("p j (l d) -> p j l d", l=LANES)
                p3 = prod[:, s]
                k = step(tt(z4, p3[:, :, :, 0], p3[:, :, :, 1], ALU.add))
                tt(p3[:, :, :, 2], p3[:, :, :, 2], v4[:, :, 0:1].to_broadcast([P, J, LANES, HD]),
                   ALU.add).then_inc(v_free, 1)
                after(k)
                dve.wait_ge(v_free, v_use[b, level] + 1)
                tt(z4, z4, p3[:, :, :, 2], ALU.add).then_inc(z_ready, 1)

            def mean_square(n):
                s = order[n][0] % 2
                dve.wait_ge(zsq_ready, n + 1)
                k = step(nc.vector.tensor_reduce(ms[:, s], z_sq[:, s].rearrange("p j (l d) -> p j l d", l=LANES),
                                                 AX, ALU.add))
                after(k)
                stt(out=arg[:, s], in0=ms[:, s], scalar=1e-8, in1=lane_sq[:], op0=ALU.add,
                    op1=ALU.mult).then_inc(arg_ready, 1)

            def normalise(n):
                s = order[n][0] % 2
                dve.wait_ge(guess_ready, n + 1)
                k = step(tt(newton[:, s], guess[:, s], guess[:, s], ALU.mult))
                after(k)
                k = step(stt(out=newton[:, s], in0=newton[:, s], scalar=-0.5, in1=arg[:, s], op0=ALU.mult, op1=ALU.mult))
                after(k)
                k = step(stt(out=root[:, s], in0=newton[:, s], scalar=1.5, in1=guess[:, s], op0=ALU.add, op1=ALU.mult))
                after(k)
                z4 = z[:, s].rearrange("p j (l d) -> p j l d", l=LANES)
                tt(z4, z4, root[:, s].rearrange("p j (l d) -> p j l d", d=1).to_broadcast([P, J, LANES, HD]),
                   ALU.mult).then_inc(scaled_ready, 1)

            for n in range(len(order)):
                made = scores(n)
                if n >= 1:
                    mean_square(n - 1)
                soften(n, made)
                if n >= 1:
                    normalise(n - 1)
                mix(n)
            mean_square(len(order) - 1)
            normalise(len(order) - 1)

            for b in range(B):
                dve.wait_ge(state_ready, order.index((b, LEVELS - 1)) + 1)
                if b >= 1:
                    dve.wait_ge(t_full, t_use["h2", b - 1] + 1)
                else:
                    dve.wait_ge(t_full, t_use["h", B - 1] + 1)
                tt(h_sb[:], q_sb[:, b], v_sb[:, b], ALU.mult).then_inc(qv_ready, 1)
                dve.wait_ge(v_full, v_use["proj", b] + 1)
                k = step(tt(centred[:], ps_v[:].rearrange("p (j c) -> p j c", j=J), rows(b, GA), ALU.mult))
                after(k)
                k = tt(x_sb[:, b], x_sb[:, b], centred[:], ALU.add).then_inc(v_free, 1)
                dve.wait_ge(v_free, v_use["proj", b] + 1)
                layernorm(B + b, b, CB, SB)

                dve.wait_ge(v_full, v_use["gate", b] + 1)
                lg = ps_v[:, 0:J * E].rearrange("p (j e) -> p j e", j=J)
                k = step(nc.vector.tensor_reduce(route_s[:, 0], lg, AX, ALU.max, negate=True))
                after(k)
                tt(logit[:], lg, route_s[:, 0].rearrange("p (j e) -> p j e", e=1).to_broadcast([P, J, E]),
                   ALU.add).then_inc(v_free, 1)
                dve.wait_ge(v_free, v_use["gate", b] + 1)
                mine = logit[:].rearrange("p j (i k) -> p j i k", k=1).to_broadcast([P, J, E, E])
                other = logit[:].rearrange("p j (i k) -> p j i k", i=1).to_broadcast([P, J, E, E])
                step(tt(beat, other, mine, ALU.is_gt))
                k = step(tt(tie, other, mine, ALU.is_equal))
                after(k)
                k = step(tt(tie, tie, before[:].rearrange("p (j i) k -> p j i k", j=1)
                            .to_broadcast([P, J, E, E]), ALU.mult))
                after(k)
                k = step(tt(beat, beat, tie, ALU.add))
                after(k)
                k = step(nc.vector.tensor_reduce(rank[:], beat, AX, ALU.add))
                after(k)
                dve.wait_ge(route_exp, b + 1)
                k = step(stt(out=rank[:], in0=rank[:], scalar=2.0, in1=route_e[:], op0=ALU.is_lt, op1=ALU.mult))
                after(k)
                k = step(nc.vector.tensor_reduce(route_s[:, 1], rank[:], AX, ALU.add))
                after(k)
                k = step(nc.vector.reciprocal(route_s[:, 2], route_s[:, 1]))
                after(k)
                wt = weight[:, b % 2]
                k = step(tt(wt, rank[:], route_s[:, 2].rearrange("p (j e) -> p j e", e=1).to_broadcast([P, J, E]),
                            ALU.mult))
                after(k)
                for half in range(2):
                    for e in range(E):
                        g = (b * 2 + half) * E + e
                        dve.wait_ge(y_full, g + 1)
                        if e >= 1:
                            dve.wait_ge(y_free, g)
                        for jj in range(4):
                            j = half * 4 + jj
                            y = ps_y[:, g % 2, jj * P:(jj + 1) * P]
                            w = wt[:, j, e:e + 1]
                            if e == 0:
                                last = ts(acc[:, j], y, w, None, ALU.mult)
                            else:
                                last = stt(out=acc[:, j], in0=y, scalar=w, in1=acc[:, j], op0=ALU.mult, op1=ALU.add)
                        last.then_inc(y_free, 1)
                dve.wait_ge(y_free, (b + 1) * 2 * E)
                k = step(tt(acc[:], acc[:], rows(b, GB), ALU.mult))
                after(k)
                tt(x_sb[:, b], acc[:], x_sb[:, b], ALU.add).then_inc(final_ready, 1)


_INS = ['L0_attn_x', 'L0_attn_W_up', 'L0_attn_W_v', 'L0_attn_W_proj', 'L0_attn_identity', 'L0_attn_W_scan_raw',
        'L0_ffn_gate_w', 'L0_ffn_w1', 'L0_ffn_w2', 'L0_c', 'L0_wmod']
_OUTS = [((4, 1024, 128), 'float32')]


def kernel(**inputs):
    import numpy as _np
    import concourse.bacc as _bacc
    from concourse import mybir as _mybir
    from concourse.bass_utils import run_bass_kernel_spmd as _run

    nc = _bacc.Bacc("TRN2", target_bir_lowering=False, num_devices=1)
    arrays, args = {}, []
    for name in _INS:
        a = _np.ascontiguousarray(inputs[name])
        arrays[f"in_{name}_dram"] = a
        args.append(nc.dram_tensor(f"in_{name}_dram", a.shape, _mybir.dt.from_np(a.dtype), kind="ExternalInput").ap())
    for i, (shape, dtype) in enumerate(_OUTS):
        dt = _mybir.dt.from_np(_np.dtype(dtype))
        args.append(nc.dram_tensor(f"out_{i}_dram", shape, dt, kind="ExternalOutput").ap())
    adaln_block(nc, *args)
    r = _run(nc, [arrays], core_ids=[0])
    got = tuple(r.results[0][f"out_{i}_dram"] for i in range(len(_OUTS)))
    return got[0]
```

```python
from contextlib import ExitStack

import concourse.bass as bass
from concourse import mybir

F32 = mybir.dt.float32
I32 = mybir.dt.int32
ALU = mybir.AluOpType
ACT = mybir.ActivationFunctionType
AX = mybir.AxisListType.X

P = 128
LANES = 4
GROW, GROW_STEPS = (3.4445, -4.7750, 2.0315), 11
POLISH, POLISH_STEPS = (1.875, -1.25, 0.375), 3
POLAR_STEPS = GROW_STEPS + POLISH_STEPS


def adaln_block(nc, x, W_up, W_v, W_proj, identity, W_scan_raw, gate_w, w1, w2, c, wmod, out):
    B, T, C = x.shape
    E, _, F = w1.shape
    J = T // P
    HD = C // LANES
    KEYS = LANES - 1
    FC = F // P
    SCALE = float(HD) ** -0.5
    LEVELS = T.bit_length() - 1
    SPLIT = 2
    STEPS_BESIDE, STEPS_AFTER = 3, 2
    SCATTERS = 4
    assert C == P and J == 8

    SLOTS = 2 * J
    PAIRS = B // 2
    BLOCKS = 2 * SLOTS + E - 1
    MOST = 2 * P * J // P
    CHUNK = 8
    CHUNKS = -(-BLOCKS // CHUNK)
    ZERO_ROWS = 13
    assert BLOCKS % ZERO_ROWS == 0

    order = [(b, n) for pair in range(0, B, 2) for n in range(LEVELS) for b in (pair, pair + 1)]
    SA, CA, GA, SB, CB, GB = range(6)

    with ExitStack() as ctx:
        def sb(name, shape, dt=F32):
            return ctx.enter_context(nc.sbuf_tensor(name, shape, dt))

        def ps(name, shape):
            return ctx.enter_context(nc.psum_tensor(name, shape, F32))

        def sem(name):
            return ctx.enter_context(nc.semaphore(name))

        eye = sb("eye", [P, P])
        eye_grow = sb("eye_grow", [P, P])
        eye_polish = sb("eye_polish", [P, P])
        ones = sb("ones", [P, P])
        w_t = sb("w_t", [P, 3, P])
        scan_raw = sb("scan_raw", [P, P])
        w_scan = sb("w_scan", [P, P])
        gate = sb("gate", [P, E])
        w1_sb = sb("w1_sb", [P, E, F])
        w2_sb = sb("w2_sb", [P, E, FC, C])
        ct = sb("ct", [P, B])
        ct_e = sb("ct_e", [P, B])
        ct_silu = sb("ct_silu", [P, B])
        mod = sb("mod", [P, B, 6, C])
        ident_row = sb("ident_row", [P // 2, C])
        ident = sb("ident", [P // 2, J, C])
        lane_sq = sb("lane_sq", [P, J, LANES])
        before = sb("before", [P, E, E])

        gram = sb("gram", [P, P])
        gram_sq = sb("gram_sq", [P, P])
        gram_t = sb("gram_t", [P, P])
        poly = sb("poly", [P, P])
        polar = sb("polar", [P, 2, P])
        norm_in = sb("norm_in", [P, 1])
        norm_ln = sb("norm_ln", [P, 1])
        norm = sb("norm", [P, 1])

        x_sb = sb("x_sb", [P, B, J, C])
        q_sb = sb("q_sb", [P, B, J, C])
        v_sb = sb("v_sb", [P, B, J, C])

        left = sb("left", [P, 2, J, C])
        both = sb("both", [P, 2, J, C])
        both_t = sb("both_t", [P, J * P])
        keys = sb("keys", [P, J, KEYS, HD])
        prod = sb("prod", [P, J, LANES, KEYS, HD])
        terms = sb("terms", [P, J, LANES, KEYS, HD])
        early = prod[:].rearrange("p j l m d -> p (j l m d)")
        wmod_sb = early[:, 0:6 * C]
        w_raw = early[:, 6 * C:6 * C + 3 * P].rearrange("p (n c) -> p n c", n=3)
        score = sb("score", [P, 2, J, LANES, LANES])
        high = sb("high", [P, 2, J, LANES])
        shifted = sb("shifted", [P, 2, J, LANES, LANES])
        expo = sb("expo", [P, 2, J, LANES, LANES])
        total = sb("total", [P, 2, J, LANES])
        recip = sb("recip", [P, 2, J, LANES])
        att = sb("att", [P, 2, J, LANES, KEYS])
        z = sb("z", [P, 2, J, C])
        z_sq = both
        ms = sb("ms", [P, 2, J, LANES])
        arg = sb("arg", [P, 2, J, LANES])
        ln_arg = sb("ln_arg", [P, 2, J, LANES])
        guess = sb("guess", [P, 2, J, LANES])
        newton = sb("newton", [P, 2, J, LANES])
        root = sb("root", [P, 2, J, LANES])

        sign, size = z[:, 0, 0:B], z[:, 0, B:2 * B]
        zeros = terms[:].rearrange("p j l m d -> p (j l m d)")[:, 0:ZERO_ROWS * C]
        h_t = sb("h_t", [P, J * P])
        stat = sb("stat", [P, B, 8, J])

        logit = sb("logit", [P, 2, J, E])
        top = sb("top", [P, J])
        beat = sb("beat", [P, J, E, E])
        tie = sb("tie", [P, J, E, E])
        rank = sb("rank", [P, J, E])
        route_e = sb("route_e", [P, 2, J, E])
        chosen = sb("chosen", [P, E, SLOTS])
        choice = sb("choice", [P, 2, E, SLOTS])
        second = sb("second", [P, 3, J])
        weight = sb("weight", [P, B, 2, J])

        upper = sb("upper", [P, P])
        none = sb("none", [P, P])
        many_i = sb("many_i", [P, MOST], I32)
        many = sb("many", [P, MOST])
        block_no_i = sb("block_no_i", [1, BLOCKS], I32)
        block_no = sb("block_no", [1, BLOCKS])
        counts = sb("counts", [P, 2, E * SLOTS])
        run_total = sb("run_total", [P, E * SLOTS])
        expert_end = sb("expert_end", [P, 1 + E])
        expert_count = sb("expert_count", [P, E])
        over = sb("over", [P, E, MOST])
        blocks_of = sb("blocks_of", [P, E])
        blocks_end = sb("blocks_end", [P, E])
        blocks_start = sb("blocks_start", [P, E])
        pad = sb("pad", [P, E])
        place = sb("place", [P, E, SLOTS])
        masked = sb("masked", [P, 2, E, SLOTS])
        row_f = sb("row_f", [P, 2, SLOTS])
        row = sb("row", [P, PAIRS, 2, SLOTS], I32)
        passed = sb("passed", [1, BLOCKS, E - 1])
        expert_f = sb("expert_f", [1, BLOCKS])
        expert_of = sb("expert_of", [1, PAIRS, BLOCKS], I32)

        rows_sb = sb("rows_sb", [P, 2, CHUNK, C])
        rows_t = sb("rows_t", [P, 2, P])
        hid = sb("hid", [P, 2, F])
        hid_t = sb("hid_t", [P, 2, FC, P])
        sorted_h = [nc.dram_tensor(f"sorted_h{i}", (BLOCKS * P, C), F32).ap() for i in range(PAIRS)]
        sorted_y = [nc.dram_tensor(f"sorted_y{i}", (BLOCKS * P, C), F32).ap() for i in range(PAIRS)]

        ps_t = ps("ps_t", [P, J * P])
        ps_v = ps("ps_v", [P, J * P])
        ps_h = ps("ps_h", [P, 2, 512])
        ps_y = ps("ps_y", [P, 2, 512])

        weights_in, polar_in, mod_in, x_in, ident_in, experts_in = (
            sem(n) for n in ("weights_in", "polar_in", "mod_in", "x_in", "ident_in", "experts_in"))
        consts = sem("consts")
        dve_const = sem("dve_const")
        ident_ready = sem("ident_ready")
        wt_done, wt_copied = sem("wt_done"), sem("wt_copied")
        silu_exp, silu_ready = sem("silu_exp"), sem("silu_ready")
        mod_done, mod_copied, mod_ready = sem("mod_done"), sem("mod_copied"), sem("mod_ready")
        gram_done, gram_copied, gram_t_ready = sem("gram_done"), sem("gram_copied"), sem("gram_t_ready")
        square_done, poly_ready = sem("square_done"), sem("poly_ready")
        next_done, next_copied, next_t_copied = sem("next_done"), sem("next_copied"), sem("next_t_copied")
        norm_sum, norm_total, norm_ready, w_scan_ready = (
            sem("norm_sum"), sem("norm_total"), sem("norm_ready"), sem("w_scan_ready"))
        t_full, t_free, v_full, v_free = sem("t_full"), sem("t_free"), sem("v_full"), sem("v_free")
        rows_t_full, rows_t_ready, hid_full, hid_ready = (
            sem("rows_t_full"), sem("rows_t_ready"), sem("hid_full"), sem("hid_ready"))
        hid_t_full, hid_t_ready, y_full, y_ready = (
            sem("hid_t_full"), sem("hid_t_ready"), sem("y_full"), sem("y_ready"))
        zeros_ready, zeroed = sem("zeros_ready"), sem("zeroed")
        rows_in, rows_out = [sem("rows_in0"), sem("rows_in1")], [sem("rows_out0"), sem("rows_out1")]
        scattered = [sem(f"scattered{i}") for i in range(PAIRS)]
        gathered = [sem(f"gathered{b}") for b in range(B)]
        centred_ready, sq_ready, var_ready, var_ln, var_exp, h_ready = (
            sem("centred_ready"), sem("sq_ready"), sem("var_ready"), sem("var_ln"), sem("var_exp"), sem("h_ready"))
        left_in = [sem("left_in0"), sem("left_in1")]
        keys_ready, both_ready, pool_prod, own_prod = (
            sem("keys_ready"), sem("both_ready"), sem("pool_prod"), sem("own_prod"))
        summed, terms_ready, pool_sum = sem("summed"), sem("terms_ready"), sem("pool_sum")
        shifted_ready, expo_ready, z_ready, zsq_ready = (
            sem("shifted_ready"), sem("expo_ready"), sem("z_ready"), sem("zsq_ready"))
        arg_ready, guess_ready, scaled_ready, half_ready, state_ready = (
            sem("arg_ready"), sem("guess_ready"), sem("scaled_ready"), sem("half_ready"), sem("state_ready"))
        qv_ready, lead_ready, route_exp, chosen_ready, place_ready = (
            sem("qv_ready"), sem("lead_ready"), sem("route_exp"), sem("chosen_ready"), sem("place_ready"))
        final_ready, stored = sem("final_ready"), sem("stored")
        dve_done, act_done, pool_done = sem("dve_done"), sem("act_done"), sem("pool_done")

        T_EARLY, V_EARLY = 3, 2
        t_use, v_use = {}, {}
        for b in range(B):
            t_use["h", b], t_use["v", b] = 2 * len(t_use) + T_EARLY, 2 * len(t_use) + T_EARLY + 2
            v_use["q", b] = len(v_use) + V_EARLY
        beside = {}

        def put(position, *item):
            beside.setdefault(position, []).append(item)

        for pair in range(PAIRS):
            b0, b1 = 2 * pair, 2 * pair + 1
            at = (pair + 1) * 2 * LEVELS - 1
            put(at, "qv", b0)
            put(at + 1, "proj", b0)
            put(at + 1, "residual", b0)
            put(at + 1, "qv", b1)
            put(at + 2, "squares", b0)
            put(at + 2, "proj", b1)
            put(at + 2, "variance", b0)
            put(at + 2, "residual", b1)
            put(at + 3, "inverse_root", b0)
            put(at + 3, "squares", b1)
            put(at + 3, "modulate", b0)
            put(at + 3, "variance", b1)
            put(at + 4, "gate", b0)
            put(at + 4, "inverse_root", b1)
            put(at + 4, "modulate", b1)
            put(at + 4, "rank", b0)
            put(at + 5, "route_exp", b0)
            put(at + 5, "gate", b1)
            put(at + 5, "weigh", b0)
            put(at + 5, "rank", b1)
            put(at + 6, "route_exp", b1)
            put(at + 6, "weigh", b1)
            put(at + 7, "count", pair)
            put(at + 7, "place", pair)
            if pair < PAIRS - 1:
                first = range(0, 2 * SLOTS, SCATTERS)
                for k, i in enumerate(first):
                    put(at + 8 + k, "scatter_early", pair, i, min(i + 2, 2 * SLOTS))
                    put(at + 8 + k, "scatter", pair, i + 2, min(i + SCATTERS, 2 * SLOTS))
                load_at = at + 8 + len(first) + 1
            else:
                put(at + 7, "scatter", pair, 0, 2 * SLOTS)
                load_at = at + 8
            put(load_at, "load", pair * CHUNKS)
            put(load_at, "load", pair * CHUNKS + 1)
            if pair == 0:
                position = load_at
        last_stage = len(order) - 1
        here = 0
        for i in range(BLOCKS + 3):
            put(position, "step", 0, i)
            here += 1
            if here == (STEPS_BESIDE if position <= last_stage else STEPS_AFTER) and position < load_at - 1:
                position, here = position + 1, 0
        last = load_at
        for i in range(BLOCKS + 3):
            put(last, "step", 1, i)
        for pair in range(PAIRS):
            for b in (2 * pair, 2 * pair + 1):
                put(last + 1 + b, "gather", b)
                put(last + 1 + b, "final", b)
        positions = max(beside) + 1

        h_users = [(("h", b), ("q", b)) for b in range(B)]
        for n in range(positions):
            if n < len(order):
                t_use[order[n]], v_use[order[n]] = 2 * len(t_use) + T_EARLY, len(v_use) + V_EARLY
            for kind, *of in beside.get(n, ()):
                if kind == "proj":
                    t_use["qv", of[0]], v_use["proj", of[0]] = 2 * len(t_use) + T_EARLY, len(v_use) + V_EARLY
                    h_users.append((("qv", of[0]), ("proj", of[0])))
                if kind == "gate":
                    t_use["h2", of[0]], v_use["gate", of[0]] = 2 * len(t_use) + T_EARLY, len(v_use) + V_EARLY
                    h_users.append((("h2", of[0]), ("gate", of[0])))
                if kind == "count":
                    v_use["count", of[0]] = len(v_use) + V_EARLY

        def run_beside(n, does):
            for kind, *of in beside.get(n, ()):
                if kind in does:
                    does[kind](*of)

        def centre_step(b):
            return 3 * b if b else 0

        def variance_step(b):
            return 3 * b + 1 if b else 1

        def scale_step(b):
            return 3 * b + 2 if b else 2

        def transpose_step(b):
            return 3 * b + 4

        LEFT_DMAS = 3

        def left_count(b, level):
            return 16 * LEFT_DMAS * sum(bb % 2 == b % 2 for bb, _ in order[:order.index((b, level)) + 1])

        block = ctx.enter_context(nc.Block())

        @block.sync
        def _(sp):
            sp.dma_start(scan_raw[:], W_scan_raw).then_inc(polar_in, 16)
            sp.dma_start(wmod_sb, wmod).then_inc(mod_in, 16)
            for b in range(B):
                sp.dma_start(x_sb[:, b], x[b].rearrange("(p j) c -> p j c", j=J)).then_inc(x_in, 16)
            sp.dma_start(w1_sb[:], w1.rearrange("e c f -> c e f")).then_inc(experts_in, 16)
            sp.dma_start(w2_sb[:], w2.rearrange("e (k p) c -> p e k c", p=P)).then_inc(experts_in, 16)

            sp.wait_ge(zeros_ready, 1)
            for pair in range(PAIRS):
                for a in range(BLOCKS // ZERO_ROWS):
                    sp.dma_start(sorted_h[pair].rearrange("(p a) c -> p (a c)", p=P)
                                 [:, a * ZERO_ROWS * C:(a + 1) * ZERO_ROWS * C], zeros).then_inc(zeroed, 16)

            sp.wait_ge(ident_ready, 1)
            for n, (b, level) in enumerate(order):
                d = 1 << level
                dst, src, mid = left[:, b % 2], q_sb[:, b], J // 2
                if level == 0:
                    sp.wait_ge(v_free, v_use["q", b] + 1)
                    if b >= 2:
                        sp.wait_ge(state_ready, order.index((b - 2, LEVELS - 1)) + 1)
                if d < J:
                    if level > 0:
                        sp.wait_ge(state_ready, order.index((b, level - 1)) + 1)
                    sp.dma_start(dst[:, d:J], src[:, 0:J - d]).then_inc(left_in[b % 2], 16)
                    sp.dma_start(dst[1:P, 0:d], src[0:P - 1, J - d:J]).then_inc(left_in[b % 2], 16)
                    sp.dma_start(dst[0:1, 0:d], ident[0:1, 0:d]).then_inc(left_in[b % 2], 16)
                else:
                    a = d // J
                    sp.wait_ge(half_ready, order.index((b, level - 1)) + 1)
                    sp.dma_start(dst[a:P, 0:mid], src[0:P - a, 0:mid]).then_inc(left_in[b % 2], 16)
                    sp.wait_ge(state_ready, order.index((b, level - 1)) + 1)
                    sp.dma_start(dst[a:P, mid:J], src[0:P - a, mid:J]).then_inc(left_in[b % 2], 16)
                    sp.dma_start(dst[0:a], ident[0:a]).then_inc(left_in[b % 2], 16)

            for b in range(B):
                sp.wait_ge(final_ready, b + 1)
                sp.dma_start(out[b].rearrange("(p j) c -> p j c", j=J), x_sb[:, b]).then_inc(stored, 16)
            sp.wait_ge(stored, 16 * B)

        @block.gpsimd
        def _(pool):
            nc.gpsimd.memset(eye[:], 0.0).then_inc(pool_done, 1)
            nc.gpsimd.memset(before[:], 0.0).then_inc(pool_done, 1)
            pool.wait_ge(pool_done, 2)
            nc.gpsimd.affine_select(out=eye[:], in_=eye[:], compare_op=ALU.not_equal, fill=1.0, base=0,
                                    pattern=[[-1, P]], channel_multiplier=1).then_inc(consts, 1)
            nc.gpsimd.affine_select(out=before[:], in_=before[:], compare_op=ALU.is_ge, fill=1.0, base=0,
                                    pattern=[[-1, E], [1, E]], channel_multiplier=0).then_inc(consts, 1)
            nc.gpsimd.memset(zeros, 0.0).then_inc(zeros_ready, 1)
            nc.gpsimd.memset(upper[:], 0.0).then_inc(pool_done, 1)
            pool.wait_ge(pool_done, 3)
            nc.gpsimd.affine_select(out=upper[:], in_=upper[:], compare_op=ALU.is_ge, fill=1.0, base=0,
                                    pattern=[[-1, P]], channel_multiplier=1).then_inc(consts, 1)
            nc.gpsimd.iota(many_i[:], [[P, MOST]], base=0, channel_multiplier=0).then_inc(consts, 1)
            nc.gpsimd.iota(block_no_i[:], [[1, BLOCKS]], base=0, channel_multiplier=0).then_inc(consts, 1)
            pool.wait_ge(ident_in, 16)
            nc.gpsimd.tensor_copy(ident[:], ident_row[:].rearrange("p (j c) -> p j c", j=1)
                                  .to_broadcast([P // 2, J, C])).then_inc(ident_ready, 1)
            tt = nc.gpsimd.tensor_tensor

            def differences(n):
                b, level = order[n]
                if level == 0:
                    pool.wait_ge(v_free, v_use["q", b] + 1)
                else:
                    pool.wait_ge(state_ready, order.index((b, level - 1)) + 1)
                if n >= 1:
                    pool.wait_ge(own_prod, n)
                    pool.wait_ge(pool_prod, n)
                q4 = q_sb[:, b].rearrange("p j (l d) -> p j l d", l=LANES)
                tt(keys[:], q4[:, :, 1:LANES, :], q4[:, :, 0:1, :].to_broadcast([P, J, KEYS, HD]),
                   ALU.subtract).then_inc(keys_ready, 1)

            def products(n):
                b, level = order[n]
                s = b % 2
                pool.wait_ge(left_in[s], left_count(b, level))
                for half in range(2):
                    at = slice(half * J // 2, (half + 1) * J // 2)
                    tt(both[:, s, at], q_sb[:, b, at], left[:, s, at], ALU.add).then_inc(both_ready, 1)
                pool.wait_ge(keys_ready, n + 1)
                if n >= 1:
                    pool.wait_ge(summed, 2 * n)
                l4 = left[:, s].rearrange("p j (l d) -> p j l d", l=LANES)
                for l in range(SPLIT, LANES):
                    last = tt(prod[:, :, l], l4[:, :, l:l + 1, :].to_broadcast([P, J, KEYS, HD]), keys[:], ALU.mult)
                last.then_inc(pool_prod, 1)

            def add_terms(n):
                s = order[n][0] % 2
                pool.wait_ge(terms_ready, n + 1)
                tt(z[:, s].rearrange("p j (l d) -> p j l d", l=LANES), terms[:, :, :, 0], terms[:, :, :, 1],
                   ALU.add).then_inc(pool_sum, 1)

            def finish(n):
                b, level = order[n]
                s = b % 2
                pool.wait_ge(scaled_ready, n + 1)
                for half, ready in ((0, half_ready), (1, state_ready)):
                    at = slice(half * J // 2, (half + 1) * J // 2)
                    tt(q_sb[:, b, at], left[:, s, at], z[:, s, at], ALU.add).then_inc(ready, 1)

            def scatter(pair, start, end):
                if start == 0:
                    pool.wait_ge(place_ready, pair + 1)
                    pool.wait_ge(zeroed, 16 * PAIRS * (BLOCKS // ZERO_ROWS))
                for n in range(start, end):
                    k, i = divmod(n, SLOTS)
                    nc.gpsimd.indirect_dma_start(
                        out=sorted_h[pair], out_offset=bass.IndirectOffsetOnAxis(ap=row[:, pair, k, i:i + 1], axis=0),
                        in_=q_sb[:, 2 * pair + i // J, i % J, :], in_offset=None,
                        bounds_check=BLOCKS * P - 1).then_inc(scattered[pair], 16)

            def gather(b):
                pair = b // 2
                for a in range(2):
                    pool.wait_ge(rows_out[a], 16 * ((CHUNKS * (pair + 1) + 1 - a) // 2))
                for k, dst in ((0, v_sb), (1, q_sb)):
                    for j in range(J):
                        i = (b % 2) * J + j
                        nc.gpsimd.indirect_dma_start(
                            out=dst[:, b, j, :], out_offset=None, in_=sorted_y[pair],
                            in_offset=bass.IndirectOffsetOnAxis(ap=row[:, pair, k, i:i + 1], axis=0),
                            bounds_check=BLOCKS * P - 1).then_inc(gathered[b], 16)

            differences(0)
            products(0)
            differences(1)
            for n in range(positions):
                if n < len(order):
                    add_terms(n)
                    if n + 1 < len(order):
                        products(n + 1)
                    run_beside(n, {"scatter_early": scatter})
                    finish(n)
                    if n + 2 < len(order):
                        differences(n + 2)
                run_beside(n, {"scatter": scatter, "gather": gather})

        @block.scalar
        def _(act):
            act.dma_start(ct[:], c.rearrange("b c -> c b"), allow_slow_non_contiguous=True).then_inc(mod_in, 16)
            act.dma_start(w_raw[:, 0], W_up).then_inc(weights_in, 16)
            act.dma_start(w_raw[:, 1], W_v).then_inc(weights_in, 16)
            act.dma_start(w_raw[:, 2], W_proj).then_inc(weights_in, 16)
            act.dma_start(gate[:], gate_w).then_inc(weights_in, 16)
            act.dma_start(ident_row[:], identity.rearrange("(a c) -> a c", a=1)
                          .to_broadcast([P // 2, C])).then_inc(ident_in, 16)
            nc.scalar.preload_act_table_set("natural_log_exp_and_others")
            act.wait_ge(mod_in, 32)
            nc.scalar.activation(ct_e[:], ct[:], ACT.Exp, scale=-1.0).then_inc(silu_exp, 1)
            def modulation_out(b):
                area, full, free = ((ps_t, t_full, t_free), (ps_v, v_full, v_free))[b % 2]
                act.wait_ge(full, b // 2 + 1)
                nc.scalar.activation(mod[:, b].rearrange("p (a m) c -> p a (m c)", a=2),
                                     area[:].rearrange("p (a n) -> p a n", a=2)[:, :, 0:3 * C],
                                     ACT.Copy).then_inc(free, 1)

            def weights_out():
                act.wait_ge(t_full, 3)
                nc.scalar.activation(w_t[:], ps_t[:, 0:3 * P].rearrange("p (n c) -> p n c", n=3),
                                     ACT.Copy).then_inc(t_free, 1)

            def evacuate(dst, key, halves=(0, 1)):
                for half in halves:
                    at = slice(half * 512, (half + 1) * 512)
                    act.wait_ge(t_full, t_use[key] + half + 1)
                    nc.scalar.activation(dst[:, at], ps_t[:, at], ACT.Copy).then_inc(t_free, 1)

            def q_out(b):
                act.wait_ge(v_full, v_use["q", b] + 1)
                nc.scalar.activation(q_sb[:, b].rearrange("p j c -> p (j c)"), ps_v[:], ACT.Copy).then_inc(v_free, 1)

            def v_out(b):
                evacuate(v_sb[:, b].rearrange("p j c -> p (j c)"), ("v", b))

            def squares(k):
                act.wait_ge(centred_ready, k + 1)
                b = k % B
                nc.scalar.activation(q_sb[:, b], v_sb[:, b], ACT.Square, scale=float(C) ** -0.5).then_inc(sq_ready, 1)

            def inverse_root(k):
                act.wait_ge(var_ready, k + 1)
                b = k % B
                nc.scalar.activation(stat[:, b, 2], stat[:, b, 1], ACT.Ln).then_inc(var_ln, 1)
                act.wait_ge(var_ln, k + 1)
                nc.scalar.activation(stat[:, b, 3], stat[:, b, 2], ACT.Exp, scale=-0.5).then_inc(var_exp, 1)

            act.wait_ge(gram_done, 1)
            nc.scalar.activation(gram_sq[:], ps_h[:, 0, 0:P], ACT.Square, accum_out=norm_in[:]).then_inc(norm_sum, 1)
            act.wait_ge(norm_total, 2)
            nc.scalar.activation(norm_ln[:], norm_in[:], ACT.Ln).then_inc(act_done, 1)
            act.wait_ge(act_done, 1)
            nc.scalar.activation(norm[:], norm_ln[:], ACT.Exp, scale=-0.25).then_inc(norm_ready, 1)
            act.wait_ge(norm_ready, 1)
            nc.scalar.activation(polar[:, 0], scan_raw[:], ACT.Copy, scale=norm[:]).then_inc(next_copied, 1)
            act.wait_ge(gram_done, 2)
            nc.scalar.activation(polar[:, 1], ps_h[:, 0, P:2 * P], ACT.Copy, scale=norm[:]).then_inc(next_t_copied, 1)
            for k in range(POLAR_STEPS):
                act.wait_ge(next_done, k + 1)
                nc.scalar.activation(polar[:, 1], ps_y[:, 1, 0:P], ACT.Copy).then_inc(next_t_copied, 1)
                if k < 2:
                    modulation_out(2 * k)
                    modulation_out(2 * k + 1)
                elif k == 2:
                    weights_out()
                for b in range(B):
                    if k == centre_step(b):
                        squares(b)
                    if k == variance_step(b):
                        inverse_root(b)
                    if k == transpose_step(b):
                        evacuate(h_t[:], ("h", b))
                    if k == transpose_step(b) + 2:
                        q_out(b)
                    if k == transpose_step(b) + 3:
                        v_out(b)
            q_out(B - 1)
            v_out(B - 1)

            def root_guess(n):
                s = order[n][0] % 2
                act.wait_ge(arg_ready, n + 1)
                nc.scalar.activation(ln_arg[:, s], arg[:, s], ACT.Ln).then_inc(act_done, 1)
                act.wait_ge(act_done, 2 * n + 2)
                nc.scalar.activation(guess[:, s], ln_arg[:, s], ACT.Exp, scale=-0.5).then_inc(act_done, 1)
                act.wait_ge(act_done, 2 * n + 3)
                nc.scalar.activation(newton[:, s], guess[:, s], ACT.Square, scale=0.5 ** 0.5).then_inc(guess_ready, 1)

            def square_out(n):
                s = order[n][0] % 2
                act.wait_ge(z_ready, n + 1)
                nc.scalar.activation(z_sq[:, s], z[:, s], ACT.Square, scale=float(HD) ** -0.5).then_inc(zsq_ready, 1)

            def transposed_out(use):
                at = [key for key, _ in h_users].index(use)
                act.wait_ge(v_full, v_use[h_users[at - 1][1]] + 1)
                evacuate(h_t, use)

            def proj(b):
                transposed_out(("qv", b))
                act.wait_ge(v_full, v_use["proj", b] + 1)
                nc.scalar.activation(v_sb[:, b].rearrange("p j c -> p (j c)"), ps_v[:], ACT.Copy).then_inc(v_free, 1)

            def gate_out(b):
                transposed_out(("h2", b))
                act.wait_ge(v_full, v_use["gate", b] + 1)
                nc.scalar.activation(logit[:, b % 2].rearrange("p j e -> p (j e)"), ps_v[:, 0:J * E],
                                     ACT.Copy).then_inc(v_free, 1)

            def exponentials(b):
                act.wait_ge(lead_ready, b + 1)
                nc.scalar.activation(route_e[:, b % 2], logit[:, b % 2], ACT.Exp).then_inc(route_exp, 1)

            def count(pair):
                act.wait_ge(v_full, v_use["count", pair] + 1)
                nc.scalar.activation(counts[:].rearrange("p a n -> p (a n)"), ps_v[:, 0:2 * E * SLOTS],
                                     ACT.Copy).then_inc(v_free, 1)

            def chunk(dram, q):
                first = (q % CHUNKS) * CHUNK
                n = min(CHUNK, BLOCKS - first)
                return (dram[q // CHUNKS][first * P:(first + n) * P].rearrange("(k p) c -> p k c", p=P),
                        rows_sb[:, q % 2, 0:n])

            def load(q):
                if q >= 2:
                    act.wait_ge(rows_out[q % 2], 16 * (q // 2))
                if q % CHUNKS < 2:
                    act.wait_ge(scattered[q // CHUNKS], 16 * 2 * SLOTS)
                src, dst = chunk(sorted_h, q)
                act.dma_start(dst, src).then_inc(rows_in[q % 2], 16)

            def store(q):
                dst, src = chunk(sorted_y, q)
                act.dma_start(dst, src).then_inc(rows_out[q % 2], 16)

            def expert_step(pair, i):
                g = pair * BLOCKS + i
                if i < BLOCKS:
                    act.wait_ge(rows_t_full, g + 1)
                    if g >= 2:
                        act.wait_ge(hid_full, g - 1)
                    nc.scalar.activation(rows_t[:, g % 2], ps_y[:, 0, 0:P], ACT.Copy).then_inc(rows_t_ready, 1)
                if 0 <= i - 1 < BLOCKS:
                    act.wait_ge(hid_full, g)
                    if g >= 3:
                        act.wait_ge(hid_t_full, g - 2)
                    nc.scalar.activation(hid[:, (g - 1) % 2], ps_h[:, 0], ACT.Gelu).then_inc(hid_ready, 1)
                if 0 <= i - 2 < BLOCKS:
                    act.wait_ge(hid_t_full, g - 1)
                    if g >= 4:
                        act.wait_ge(y_full, g - 3)
                    nc.scalar.activation(hid_t[:, g % 2].rearrange("p f t -> p (f t)"), ps_h[:, 1],
                                         ACT.Copy).then_inc(hid_t_ready, 1)
                if 0 <= i - 3 < BLOCKS:
                    act.wait_ge(y_full, g - 2)
                    c, k = divmod(i - 3, CHUNK)
                    q = pair * CHUNKS + c
                    nc.scalar.activation(rows_sb[:, q % 2, k], ps_y[:, 1, 0:C], ACT.Copy).then_inc(y_ready, 1)
                    if k == CHUNK - 1 or i - 3 == BLOCKS - 1:
                        act.wait_ge(y_ready, g - 2)
                        store(q)
                c, k = divmod(i, CHUNK)
                if k == 5 and 2 <= c + 1 < CHUNKS:
                    load(pair * CHUNKS + c + 1)

            for n in range(positions):
                if n == len(order):
                    square_out(n - 1)
                    root_guess(n - 1)
                if n < len(order):
                    b, level = order[n]
                    s = b % 2
                    if n >= 1:
                        square_out(n - 1)
                        act.wait_ge(v_full, v_use[order[n - 1]] + 1)
                    evacuate(both_t, (b, level))
                    if n >= 1:
                        root_guess(n - 1)
                    act.wait_ge(shifted_ready, n + 1)
                    nc.scalar.activation(expo[:, s], shifted[:, s], ACT.Exp, scale=SCALE).then_inc(expo_ready, 1)
                run_beside(n, {"proj": proj, "squares": lambda b: squares(B + b), "gate": gate_out,
                               "inverse_root": lambda b: inverse_root(B + b), "route_exp": exponentials,
                               "count": count, "load": load, "step": expert_step})
                if any(kind == "step" for kind, *_ in beside.get(n, ())):
                    nc.scalar.preload_act_table_set("natural_log_exp_and_others")

        @block.tensor
        def _(pe):
            def transposes(src, key, ready=None):
                pe.wait_ge(t_free, t_use[key])
                for half in range(2):
                    if ready is not None:
                        pe.wait_ge(*ready[half])
                    for j in range(half * J // 2, (half + 1) * J // 2):
                        last = nc.tensor.transpose(ps_t[:, j * P:(j + 1) * P], src[:, j], eye[:])
                    last.then_inc(t_full, 1)

            def products(src_t, rhs, key, width, t_key):
                pe.wait_ge(v_free, v_use[key])
                for j in range(J):
                    if j % (J // 2) == 0:
                        pe.wait_ge(t_free, t_use[t_key] + j // (J // 2) + 1)
                    last = nc.tensor.matmul(ps_v[:, j * width:(j + 1) * width], src_t[:, j * P:(j + 1) * P], rhs,
                                            start=True, stop=True)
                last.then_inc(v_full, 1)

            def modulation(b):
                area, full, free = ((ps_t, t_full, t_free), (ps_v, v_full, v_free))[b % 2]
                if b == 0:
                    pe.wait_ge(silu_ready, 1)
                if b >= 2:
                    pe.wait_ge(free, 1)
                for a in range(2):
                    last = nc.tensor.matmul(area[:, a * 512:a * 512 + 3 * C], ct_silu[:, b:b + 1].to_broadcast([P, P]),
                                            wmod_sb[:, a * 3 * C:(a + 1) * 3 * C], start=True, stop=True)
                last.then_inc(full, 1)

            def weights():
                pe.wait_ge(weights_in, 64)
                pe.wait_ge(t_free, 2)
                for n in range(3):
                    last = nc.tensor.transpose(ps_t[:, n * P:(n + 1) * P], w_raw[:, n], eye[:])
                last.then_inc(t_full, 1)

            def qv_piece(b, i):
                if i == 0:
                    pe.wait_ge(v_free, v_use["q", b])
                    pe.wait_ge(t_free, t_use["h", b] + 2)
                if i < 8:
                    area, full = (ps_v, v_full) if i < 4 else (ps_t, t_full)
                    for j in (2 * (i % 4), 2 * (i % 4) + 1):
                        last = nc.tensor.matmul(area[:, j * P:(j + 1) * P], h_t[:, j * P:(j + 1) * P], w_t[:, i // 4],
                                                start=True, stop=True)
                    if i == 3 or i >= 4 and i % 2:
                        last.then_inc(full, 1)

            def beside(k, gap):
                if gap == 2 and k < 2:
                    modulation(2 * k)
                    modulation(2 * k + 1)
                if gap == 2 and k == 2:
                    weights()
                for b in range(B):
                    if gap == 2 and k == transpose_step(b):
                        pe.wait_ge(h_ready, b + 1)
                        transposes(q_sb[:, b], ("h", b))
                    i = 3 * (k - transpose_step(b) - 1) + gap
                    if 0 <= i < 9:
                        qv_piece(b, i)

            pe.wait_ge(polar_in, 16)
            nc.tensor.matmul(ps_h[:, 0, 0:P], scan_raw[:], scan_raw[:], start=True, stop=True).then_inc(gram_done, 1)
            pe.wait_ge(norm_sum, 1)
            pe.wait_ge(dve_const, 3)
            nc.tensor.matmul(ps_h[:, 1, 0:1], ones[:], norm_in[:], start=True, stop=True).then_inc(norm_total, 1)
            pe.wait_ge(consts, 2)
            nc.tensor.transpose(ps_h[:, 0, P:2 * P], scan_raw[:], eye[:]).then_inc(gram_done, 1)
            for k in range(POLAR_STEPS):
                pe.wait_ge(next_copied, k + 1)
                pe.wait_ge(next_t_copied, k + 1)
                nc.tensor.matmul(ps_h[:, 0, 0:P], polar[:, 0], polar[:, 0], start=True, stop=True).then_inc(gram_done, 1)
                beside(k, 0)
                pe.wait_ge(gram_copied, k + 1)
                nc.tensor.matmul(ps_h[:, 1, 0:P], gram[:], gram[:], start=True, stop=True).then_inc(square_done, 1)
                beside(k, 1)
                pe.wait_ge(poly_ready, k + 1)
                nc.tensor.matmul(ps_y[:, 0, 0:P], polar[:, 1], poly[:], start=True, stop=True)
                nc.tensor.matmul(ps_y[:, 1, 0:P], poly[:], polar[:, 1], start=True, stop=True).then_inc(next_done, 1)
                beside(k, 2)
            for gap in range(9):
                beside(POLAR_STEPS + gap // 3, gap % 3)

            pe.wait_ge(w_scan_ready, 1)
            def proj(b):
                pe.wait_ge(qv_ready, b + 1)
                transposes(q_sb[:, b], ("qv", b))
                products(h_t, w_t[:, 2], ("proj", b), C, ("qv", b))

            def gate_products(b):
                pe.wait_ge(h_ready, B + b + 1)
                transposes(q_sb[:, b], ("h2", b))
                products(h_t, gate[:], ("gate", b), E, ("h2", b))

            def count(pair):
                pe.wait_ge(chosen_ready, 2 * pair + 2)
                pe.wait_ge(v_free, v_use["count", pair])
                each = chosen[:].rearrange("p e i -> p (e i)")
                nc.tensor.matmul(ps_v[:, 0:E * SLOTS], upper[:], each, start=True, stop=True)
                nc.tensor.matmul(ps_v[:, E * SLOTS:2 * E * SLOTS], ones[:], each, start=True,
                                 stop=True).then_inc(v_full, 1)

            def expert(pair, i):
                return nc.tensor.value_load(expert_of[0:1, pair, i:i + 1], min_val=0, max_val=E - 1)

            def expert_step(pair, i):
                g = pair * BLOCKS + i
                if i < BLOCKS:
                    c, k = divmod(i, CHUNK)
                    q = pair * CHUNKS + c
                    if k == 0:
                        pe.wait_ge(rows_in[q % 2], 16 * (q // 2 + 1))
                    if i == 0:
                        pe.wait_ge(place_ready, pair + 1)
                        pe.wait_ge(experts_in, 32)
                    if g >= 1:
                        pe.wait_ge(rows_t_ready, g)
                    nc.tensor.transpose(ps_y[:, 0, 0:P], rows_sb[:, q % 2, k], eye[:]).then_inc(rows_t_full, 1)
                if 0 <= i - 1 < BLOCKS:
                    e = expert(pair, i - 1)
                    pe.wait_ge(rows_t_ready, g)
                    if g >= 2:
                        pe.wait_ge(hid_ready, g - 1)
                    nc.tensor.matmul(ps_h[:, 0], rows_t[:, (g - 1) % 2], w1_sb[:, bass.ds(e, 1), :]
                                     .rearrange("p a f -> p (a f)"), start=True, stop=True).then_inc(hid_full, 1)
                if 0 <= i - 2 < BLOCKS:
                    pe.wait_ge(hid_ready, g - 1)
                    if g >= 3:
                        pe.wait_ge(hid_t_ready, g - 2)
                    for f in range(FC):
                        last = nc.tensor.transpose(ps_h[:, 1, f * P:(f + 1) * P], hid[:, g % 2, f * P:(f + 1) * P],
                                                   eye[:])
                    last.then_inc(hid_t_full, 1)
                if 0 <= i - 3 < BLOCKS:
                    e = expert(pair, i - 3)
                    pe.wait_ge(hid_t_ready, g - 2)
                    if g >= 4:
                        pe.wait_ge(y_ready, g - 3)
                    for f in range(FC):
                        last = nc.tensor.matmul(ps_y[:, 1, 0:C], hid_t[:, (g - 3) % 2, f],
                                                w2_sb[:, bass.ds(e, 1), f, :].rearrange("p a c -> p (a c)"),
                                                start=(f == 0), stop=(f == FC - 1))
                    last.then_inc(y_full, 1)

            for n in range(positions):
                if n < len(order):
                    b, level = order[n]
                    transposes(both[:, b % 2], (b, level), [(both_ready, 2 * n + 1), (both_ready, 2 * n + 2)])
                    products(both_t, w_scan[:], (b, level), C, (b, level))
                run_beside(n, {"proj": proj, "gate": gate_products, "count": count, "step": expert_step})

        @block.vector
        def _(dve):
            count = [0]

            def step(ins):
                ins.then_inc(dve_done, 1)
                count[0] += 1
                return count[0]

            def after(n):
                dve.wait_ge(dve_done, n)

            tt, ts, stt = nc.vector.tensor_tensor, nc.vector.tensor_scalar, nc.vector.scalar_tensor_tensor
            nc.vector.memset(ones[:], 1.0).then_inc(dve_const, 1)
            for l in range(LANES):
                last = nc.vector.memset(lane_sq[:, :, l:l + 1], float((l + 1) ** 2))
            last.then_inc(dve_const, 1)
            dve.wait_ge(consts, 1)
            after(step(ts(eye_grow[:], eye[:], GROW[0], None, ALU.mult)))
            ts(eye_polish[:], eye[:], POLISH[0], None, ALU.mult).then_inc(dve_const, 1)

            nc.vector.memset(none[:], 0.0)
            nc.vector.memset(score[:], 0.0)
            nc.vector.memset(expert_end[:], 0.0)
            dve.wait_ge(consts, 5)
            nc.vector.tensor_copy(many[:], many_i[:])
            after(step(nc.vector.tensor_copy(block_no[:], block_no_i[:])))

            dve.wait_ge(silu_exp, 1)
            k = step(ts(ct_e[:], ct_e[:], 1.0, None, ALU.add))
            after(k)
            k = step(nc.vector.reciprocal(ct_e[:], ct_e[:]))
            after(k)
            tt(ct_silu[:], ct[:], ct_e[:], ALU.mult).then_inc(silu_ready, 1)

            dve.wait_ge(dve_const, 3)
            dve.wait_ge(norm_total, 1)
            ts(norm_in[:], ps_h[:, 1, 0:1], 1e-18, None, ALU.max).then_inc(norm_total, 1)
            def rows(b, m):
                return mod[:, b, m:m + 1, :].to_broadcast([P, J, C])

            def per_token(a):
                return a.rearrange("p (j c) -> p j c", c=1).to_broadcast([P, J, C])

            def centre(k, b):
                n = step(nc.vector.tensor_reduce(stat[:, b, 0], x_sb[:, b], AX, ALU.add))
                after(n)
                stt(out=v_sb[:, b], in0=per_token(stat[:, b, 0]), scalar=-1.0 / C, in1=x_sb[:, b], op0=ALU.mult,
                    op1=ALU.add).then_inc(centred_ready, 1)

            def variance(k, b):
                dve.wait_ge(sq_ready, k + 1)
                n = step(nc.vector.tensor_reduce(stat[:, b, 4], q_sb[:, b], AX, ALU.add))
                after(n)
                ts(stat[:, b, 1], stat[:, b, 4], 1e-5, None, ALU.add).then_inc(var_ready, 1)

            def modulate(k, b, scale_row, shift_row):
                dve.wait_ge(var_exp, k + 1)
                st = stat[:, b]
                n = step(tt(st[:, 5], st[:, 3], st[:, 3], ALU.mult))
                after(n)
                n = step(stt(out=st[:, 6], in0=st[:, 5], scalar=-0.5, in1=st[:, 1], op0=ALU.mult, op1=ALU.mult))
                after(n)
                n = step(stt(out=st[:, 7], in0=st[:, 6], scalar=1.5, in1=st[:, 3], op0=ALU.add, op1=ALU.mult))
                after(n)
                n = step(tt(v_sb[:, b], v_sb[:, b], per_token(st[:, 7]), ALU.mult))
                after(n)
                n = step(tt(v_sb[:, b], v_sb[:, b], rows(b, scale_row), ALU.mult))
                after(n)
                tt(q_sb[:, b], v_sb[:, b], rows(b, shift_row), ALU.add).then_inc(h_ready, 1)

            def scale_rows():
                for m in (CA, CB):
                    n = step(ts(mod[:, :, m], mod[:, :, m], 1.0, None, ALU.add))
                after(n)

            def gate_rows():
                for m in (GA, GB):
                    n = step(ts(sign, mod[:, :, m], 0.0, 2.0, ALU.is_ge, ALU.mult))
                    n = step(stt(out=size, in0=mod[:, :, m], scalar=-1.0, in1=mod[:, :, m], op0=ALU.mult, op1=ALU.max))
                    after(n)
                    n = step(ts(size, size, 0.25, None, ALU.max))
                    after(n)
                    n = step(stt(out=mod[:, :, m], in0=sign, scalar=-1.0, in1=size, op0=ALU.add, op1=ALU.mult))
                    after(n)

            for k in range(POLAR_STEPS):
                grow = k < GROW_STEPS
                (_, cb, cc), eye_a = (GROW, eye_grow) if grow else (POLISH, eye_polish)
                dve.wait_ge(gram_done, k + 3)
                nc.vector.tensor_copy(gram[:], ps_h[:, 0, 0:P]).then_inc(gram_copied, 1)
                stt(out=gram_t[:], in0=ps_h[:, 0, 0:P], scalar=cb, in1=eye_a[:], op0=ALU.mult,
                    op1=ALU.add).then_inc(gram_t_ready, 1)
                dve.wait_ge(square_done, k + 1)
                dve.wait_ge(gram_t_ready, k + 1)
                stt(out=poly[:], in0=ps_h[:, 1, 0:P], scalar=cc, in1=gram_t[:], op0=ALU.mult,
                    op1=ALU.add).then_inc(poly_ready, 1)
                dve.wait_ge(next_done, k + 1)
                nc.vector.tensor_copy(polar[:, 0], ps_y[:, 0, 0:P]).then_inc(next_copied, 1)
                if k == 2:
                    dve.wait_ge(t_free, 2)
                    dve.wait_ge(v_free, 2)
                    scale_rows()
                for b in range(B):
                    if k == centre_step(b):
                        dve.wait_ge(x_in, 16 * B)
                        centre(b, b)
                    if k == variance_step(b):
                        variance(b, b)
                    if k == scale_step(b):
                        modulate(b, b, CA, SA)
            dve.wait_ge(next_copied, GROW_STEPS + POLISH_STEPS + 1)
            nc.vector.tensor_copy(w_scan[:, 0:HD], polar[:, 0, 0:HD])
            tt(w_scan[:, HD:].rearrange("p (m d) -> p m d", d=HD), polar[:, 0, HD:].rearrange("p (m d) -> p m d", d=HD),
               polar[:, 0, 0:HD].rearrange("p (m d) -> p m d", m=1).to_broadcast([P, KEYS, HD]),
               ALU.subtract).then_inc(w_scan_ready, 1)

            gate_rows()
            dve.wait_ge(zeroed, 16 * PAIRS * (BLOCKS // ZERO_ROWS))

            def scores(n):
                b, level = order[n]
                s = b % 2
                dve.wait_ge(keys_ready, n + 1)
                dve.wait_ge(left_in[s], left_count(b, level))
                l4 = left[:, s].rearrange("p j (l d) -> p j l d", l=LANES)
                for l in range(SPLIT):
                    last = tt(prod[:, :, l], l4[:, :, l:l + 1, :].to_broadcast([P, J, KEYS, HD]), keys[:], ALU.mult)
                last.then_inc(own_prod, 1)

            def join(n):
                s = order[n][0] % 2
                dve.wait_ge(pool_sum, n + 1)
                dve.wait_ge(v_free, v_use[order[n]] + 1)
                z4 = z[:, s].rearrange("p j (l d) -> p j l d", l=LANES)
                tt(z4, z4, terms[:, :, :, 2], ALU.add).then_inc(z_ready, 1)

            def sum_products(n, own):
                s = order[n][0] % 2
                dve.wait_ge(own_prod if own else pool_prod, n + 1)
                lanes = slice(0, SPLIT) if own else slice(SPLIT, LANES)
                nc.vector.tensor_reduce(score[:, s, :, lanes, 1:], prod[:, :, lanes], AX, ALU.add).then_inc(summed, 1)

            def mean_square(n):
                o = order[n][0] % 2
                dve.wait_ge(zsq_ready, n + 1)
                return step(nc.vector.tensor_reduce(ms[:, o], z_sq[:, o].rearrange("p j (l d) -> p j l d", l=LANES),
                                                    AX, ALU.add))

            def root_argument(n, k):
                o = order[n][0] % 2
                after(k)
                stt(out=arg[:, o], in0=ms[:, o], scalar=1e-8, in1=lane_sq[:], op0=ALU.add,
                    op1=ALU.mult).then_inc(arg_ready, 1)

            def soften(n):
                s = order[n][0] % 2
                dve.wait_ge(summed, 2 * n + 2)
                k = step(nc.vector.tensor_reduce(high[:, s], score[:, s], AX, ALU.max))
                after(k)
                tt(shifted[:, s], score[:, s], high[:, s].rearrange("p j (l m) -> p j l m", m=1)
                   .to_broadcast([P, J, LANES, LANES]), ALU.subtract).then_inc(shifted_ready, 1)

            def normalise(n):
                s = order[n][0] % 2
                dve.wait_ge(guess_ready, n + 1)
                k = step(stt(out=newton[:, s], in0=newton[:, s], scalar=-1.0, in1=arg[:, s], op0=ALU.mult, op1=ALU.mult))
                after(k)
                k = step(stt(out=root[:, s], in0=newton[:, s], scalar=1.5, in1=guess[:, s], op0=ALU.add, op1=ALU.mult))
                after(k)
                z4 = z[:, s].rearrange("p j (l d) -> p j l d", l=LANES)
                tt(z4, z4, root[:, s].rearrange("p j (l d) -> p j l d", d=1).to_broadcast([P, J, LANES, HD]),
                   ALU.mult).then_inc(scaled_ready, 1)

            def mix(n):
                b, level = order[n]
                s = b % 2
                dve.wait_ge(expo_ready, n + 1)
                k = step(nc.vector.tensor_reduce(total[:, s], expo[:, s], AX, ALU.add))
                after(k)
                k = step(nc.vector.reciprocal(recip[:, s], total[:, s]))
                after(k)
                k = step(tt(att[:, s], expo[:, s, :, :, 1:], recip[:, s].rearrange("p j (l m) -> p j l m", m=1)
                            .to_broadcast([P, J, LANES, KEYS]), ALU.mult))
                after(k)
                dve.wait_ge(v_full, v_use[b, level] + 1)
                v4 = ps_v[:].rearrange("p (j m d) -> p j m d", m=LANES, d=HD)
                for m in range(KEYS):
                    last = tt(terms[:, :, :, m], att[:, s, :, :, m:m + 1].to_broadcast([P, J, LANES, HD]),
                              v4[:, :, 1 + m:2 + m].to_broadcast([P, J, LANES, HD]), ALU.mult)
                    if m == 1:
                        last.then_inc(terms_ready, 1)
                after(step(last))
                tt(terms[:, :, :, 2], terms[:, :, :, 2], v4[:, :, 0:1].to_broadcast([P, J, LANES, HD]),
                   ALU.add).then_inc(v_free, 1)

            def qv(b):
                dve.wait_ge(state_ready, order.index((b, LEVELS - 1)) + 1)
                tt(q_sb[:, b], q_sb[:, b], v_sb[:, b], ALU.mult).then_inc(qv_ready, 1)

            def residual(b):
                dve.wait_ge(v_free, v_use["proj", b] + 1)
                k = step(tt(v_sb[:, b], v_sb[:, b], rows(b, GA), ALU.mult))
                after(k)
                k = step(tt(x_sb[:, b], x_sb[:, b], v_sb[:, b], ALU.add))
                after(k)
                centre(B + b, b)

            def rank_experts(b):
                lg, s = logit[:, b % 2], b % 2
                dve.wait_ge(v_free, v_use["gate", b] + 1)
                k = step(nc.vector.tensor_reduce(top[:], lg, AX, ALU.max, negate=True))
                mine = lg.rearrange("p j (i k) -> p j i k", k=1).to_broadcast([P, J, E, E])
                other = lg.rearrange("p j (i k) -> p j i k", i=1).to_broadcast([P, J, E, E])
                step(tt(beat[:], other, mine, ALU.is_gt))
                k = step(tt(tie[:], other, mine, ALU.is_equal))
                after(k)
                tt(lg, lg, top[:].rearrange("p (j e) -> p j e", e=1).to_broadcast([P, J, E]),
                   ALU.add).then_inc(lead_ready, 1)
                k = step(tt(tie[:], tie[:], before[:].rearrange("p (j i) k -> p j i k", j=1)
                            .to_broadcast([P, J, E, E]), ALU.mult))
                after(k)
                k = step(tt(beat[:], beat[:], tie[:], ALU.add))
                after(k)
                k = step(nc.vector.tensor_reduce(rank[:], beat[:], AX, ALU.add))
                after(k)
                at = slice(s * J, (s + 1) * J)
                by_expert = rank[:].rearrange("p j e -> p e j")
                step(ts(choice[:, 0, :, at], by_expert, 1.0, None, ALU.is_lt))
                k = step(ts(chosen[:, :, at], by_expert, 2.0, None, ALU.is_lt))
                after(k)
                tt(choice[:, 1, :, at], chosen[:, :, at], choice[:, 0, :, at], ALU.subtract).then_inc(chosen_ready, 1)

            def weigh(b):
                s = b % 2
                at = slice(s * J, (s + 1) * J)
                dve.wait_ge(chosen_ready, b + 1)
                dve.wait_ge(route_exp, b + 1)
                k = step(tt(rank[:], choice[:, 1, :, at].rearrange("p e j -> p j e"), route_e[:, s], ALU.mult))
                after(k)
                k = step(nc.vector.tensor_reduce(second[:, 0], rank[:], AX, ALU.add))
                after(k)
                k = step(ts(second[:, 1], second[:, 0], 1.0, None, ALU.add))
                after(k)
                k = step(nc.vector.reciprocal(weight[:, b, 0], second[:, 1]))
                after(k)
                step(tt(weight[:, b, 1], second[:, 0], weight[:, b, 0], ALU.mult))

            def place_rows(pair):
                dve.wait_ge(v_free, v_use["count", pair] + 1)
                k = step(nc.vector.tensor_tensor_scan(run_total[:], counts[:, 1], none[:, 0:E * SLOTS], 0.0, ALU.add,
                                                      ALU.add))
                after(k)
                by_slot = run_total[:].rearrange("p (e i) -> p e i", e=E)
                k = step(nc.vector.tensor_copy(expert_end[:, 1:], by_slot[:, :, SLOTS - 1]))
                flat = place[:].rearrange("p e i -> p (e i)")
                m = step(tt(flat, run_total[:], counts[:, 1], ALU.subtract))
                after(k)
                k = step(tt(expert_count[:], expert_end[:, 1:], expert_end[:, 0:E], ALU.subtract))
                after(m)
                step(tt(flat, flat, counts[:, 0], ALU.add))
                after(k)
                k = step(tt(over[:], expert_count[:].rearrange("p (e n) -> p e n", n=1).to_broadcast([P, E, MOST]),
                            many[:].rearrange("p (e n) -> p e n", e=1).to_broadcast([P, E, MOST]), ALU.is_gt))
                after(k)
                k = step(nc.vector.tensor_reduce(blocks_of[:], over[:], AX, ALU.add))
                after(k)
                k = step(nc.vector.tensor_tensor_scan(blocks_end[:], blocks_of[:], none[:, 0:E], 0.0, ALU.add, ALU.add))
                after(k)
                k = step(tt(blocks_start[:], blocks_end[:], blocks_of[:], ALU.subtract))
                m = step(tt(passed[:], block_no[:].rearrange("p (n e) -> p n e", e=1).to_broadcast([1, BLOCKS, E - 1]),
                            blocks_end[0:1, 0:E - 1].rearrange("p (n e) -> p n e", n=1)
                            .to_broadcast([1, BLOCKS, E - 1]), ALU.is_ge))
                after(k)
                k = step(stt(out=pad[:], in0=blocks_start[:], scalar=float(P), in1=expert_end[:, 0:E], op0=ALU.mult,
                             op1=ALU.subtract))
                after(m)
                m = step(nc.vector.tensor_reduce(expert_f[:], passed[:], AX, ALU.add))
                after(k)
                k = step(tt(place[:], place[:], pad[:].rearrange("p (e i) -> p e i", i=1)
                            .to_broadcast([P, E, SLOTS]), ALU.add))
                after(m)
                step(nc.vector.tensor_copy(expert_of[:, pair], expert_f[:]))
                after(k)
                k = step(tt(masked[:], choice[:], place[:].rearrange("p (a e) i -> p a e i", a=1)
                            .to_broadcast([P, 2, E, SLOTS]), ALU.mult))
                after(k)
                k = step(nc.vector.tensor_reduce(row_f[:], masked[:].rearrange("p a e i -> p a i e"), AX, ALU.add))
                after(k)
                nc.vector.tensor_copy(row[:, pair], row_f[:]).then_inc(place_ready, 1)

            def final(b):
                dve.wait_ge(gathered[b], 16 * 2 * J)
                step(tt(v_sb[:, b], v_sb[:, b], per_token(weight[:, b, 0]), ALU.mult))
                k = step(tt(q_sb[:, b], q_sb[:, b], per_token(weight[:, b, 1]), ALU.mult))
                after(k)
                k = step(tt(v_sb[:, b], v_sb[:, b], q_sb[:, b], ALU.add))
                after(k)
                k = step(tt(v_sb[:, b], v_sb[:, b], rows(b, GB), ALU.mult))
                after(k)
                tt(x_sb[:, b], v_sb[:, b], x_sb[:, b], ALU.add).then_inc(final_ready, 1)

            for n in range(positions):
                if n < len(order):
                    scores(n)
                if 1 <= n <= len(order):
                    k = mean_square(n - 1)
                    root_argument(n - 1, k)
                if n < len(order):
                    sum_products(n, own=True)
                if 1 <= n <= len(order):
                    normalise(n - 1)
                if n < len(order):
                    sum_products(n, own=False)
                    soften(n)
                    mix(n)
                    join(n)
                run_beside(n, {"qv": qv, "residual": residual, "variance": lambda b: variance(B + b, b),
                               "modulate": lambda b: modulate(B + b, b, CB, SB), "rank": rank_experts,
                               "weigh": weigh, "place": place_rows, "final": final})


_INS = ['L0_attn_x', 'L0_attn_W_up', 'L0_attn_W_v', 'L0_attn_W_proj', 'L0_attn_identity', 'L0_attn_W_scan_raw',
        'L0_ffn_gate_w', 'L0_ffn_w1', 'L0_ffn_w2', 'L0_c', 'L0_wmod']
_OUTS = [((4, 1024, 128), 'float32')]


def kernel(**inputs):
    import numpy as _np
    import concourse.bacc as _bacc
    from concourse import mybir as _mybir
    from concourse.bass_utils import run_bass_kernel_spmd as _run

    nc = _bacc.Bacc("TRN2", target_bir_lowering=False, num_devices=1)
    arrays, args = {}, []
    for name in _INS:
        a = _np.ascontiguousarray(inputs[name])
        arrays[f"in_{name}_dram"] = a
        args.append(nc.dram_tensor(f"in_{name}_dram", a.shape, _mybir.dt.from_np(a.dtype), kind="ExternalInput").ap())
    for i, (shape, dtype) in enumerate(_OUTS):
        dt = _mybir.dt.from_np(_np.dtype(dtype))
        args.append(nc.dram_tensor(f"out_{i}_dram", shape, dt, kind="ExternalOutput").ap())
    adaln_block(nc, *args)
    r = _run(nc, [arrays], core_ids=[0])
    got = tuple(r.results[0][f"out_{i}_dram"] for i in range(len(_OUTS)))
    return got[0]
```

```python
from contextlib import ExitStack

import concourse.bass as bass
from concourse import mybir

F32 = mybir.dt.float32
I32 = mybir.dt.int32
ALU = mybir.AluOpType
ACT = mybir.ActivationFunctionType
AX = mybir.AxisListType.X

P = 128
LANES = 4
GROW, GROW_STEPS = (3.4445, -4.7750, 2.0315), 11
POLISH, POLISH_STEPS = (1.875, -1.25, 0.375), 3
POLAR_STEPS = GROW_STEPS + POLISH_STEPS


def adaln_block(nc, x, W_up, W_v, W_proj, identity, W_scan_raw, gate_w, w1, w2, c, wmod, out):
    B, T, C = x.shape
    E, _, F = w1.shape
    J = T // P
    HD = C // LANES
    KEYS = LANES - 1
    FC = F // P
    SCALE = float(HD) ** -0.5
    LEVELS = T.bit_length() - 1
    SPLIT = 1
    OTHERS = LANES - SPLIT
    STEPS_BESIDE, STEPS_AFTER = 2, 0
    SCATTERS = 5
    assert C == P and J == 8

    SLOTS = 2 * J
    PAIRS = B // 2
    BLOCKS = 2 * SLOTS + E - 1
    MOST = 2 * P * J // P
    CHUNK, BUFFERS = 4, 4
    CHUNKS = -(-BLOCKS // CHUNK)
    WIDE = C + 2
    BACK_ROWS = 2 * SLOTS * P
    EMPTY_BLOCKS = -(-BLOCKS // 2)
    assert EMPTY_BLOCKS > BUFFERS * CHUNK

    order = [(b, n) for pair in range(0, B, 2) for n in range(LEVELS) for b in (pair, pair + 1)]
    SA, CA, GA, SB, CB, GB = range(6)

    with ExitStack() as ctx:
        def sb(name, shape, dt=F32):
            return ctx.enter_context(nc.sbuf_tensor(name, shape, dt))

        def ps(name, shape):
            return ctx.enter_context(nc.psum_tensor(name, shape, F32))

        def sem(name):
            return ctx.enter_context(nc.semaphore(name))

        eye = sb("eye", [P, P])
        eye_grow = sb("eye_grow", [P, P])
        eye_polish = sb("eye_polish", [P, P])
        ones = sb("ones", [P, P])
        w_t = sb("w_t", [P, 3, P])
        scan_raw = sb("scan_raw", [P, P])
        w_scan = sb("w_scan", [P, P])
        gate = sb("gate", [P, E])
        w1_sb = sb("w1_sb", [P, E, F])
        w2_sb = sb("w2_sb", [P, E, FC, C])
        ct = sb("ct", [P, B])
        ct_e = sb("ct_e", [P, B])
        ct_silu = sb("ct_silu", [P, B])
        mod = sb("mod", [P, B, 6, C])
        ident_row = sb("ident_row", [P // 2, C])
        ident = ident_row[:].rearrange("p (j c) -> p j c", j=1).to_broadcast([P // 2, J, C])
        lane_sq = sb("lane_sq", [P, J, LANES])
        early_first = sb("early_first", [P, E])

        gram = sb("gram", [P, P])
        gram_sq = sb("gram_sq", [P, P])
        gram_t = sb("gram_t", [P, P])
        poly = sb("poly", [P, P])
        polar = sb("polar", [P, 2, P])
        norm_in = sb("norm_in", [P, 1])
        norm_ln = sb("norm_ln", [P, 1])
        norm = sb("norm", [P, 1])

        x_sb = sb("x_sb", [P, B, J, C])
        q_sb = sb("q_sb", [P, B, J, C])
        v_sb = sb("v_sb", [P, B, J, C])

        left = sb("left", [P, 2, J, C])
        both_t = sb("both_t", [P, J * P])
        keys = sb("keys", [P, J, KEYS, HD])
        prod = sb("prod", [P, J, LANES, KEYS, HD])
        terms = sb("terms", [P, J, LANES, KEYS, HD])
        early = prod[:].rearrange("p j l m d -> p (j l m d)")
        wmod_sb = early[:, 0:6 * C]
        w_raw = early[:, 6 * C:6 * C + 3 * P].rearrange("p (n c) -> p n c", n=3)
        score = sb("score", [P, 2, J, LANES, LANES])
        high = sb("high", [P, 2, J, LANES])
        shifted = sb("shifted", [P, 2, J, LANES, LANES])
        expo = sb("expo", [P, 2, J, LANES, LANES])
        total = sb("total", [P, 2, J, LANES])
        recip = sb("recip", [P, 2, J, LANES])
        att = sb("att", [P, 2, J, LANES, KEYS])
        z = sb("z", [P, 2, J, C])
        z_sq = sb("z_sq", [P, J, C])
        ms = sb("ms", [P, 2, J, LANES])
        arg = sb("arg", [P, 2, J, LANES])
        ln_arg = sb("ln_arg", [P, 2, J, LANES])
        guess = sb("guess", [P, 2, J, LANES])
        newton = sb("newton", [P, 2, J, LANES])
        root = sb("root", [P, 2, J, LANES])

        sign, size = z[:, 0, 0:B], z[:, 0, B:2 * B]
        empty = terms[:].rearrange("p j l m d -> p (j l m d)")[:, 0:EMPTY_BLOCKS * WIDE].rearrange(
            "p (a c) -> p a c", c=WIDE)
        h_t = sb("h_t", [P, J * P])
        stat = sb("stat", [P, B, 8, J])

        logit = sb("logit", [P, 2, SLOTS, E])
        top = sb("top", [P, 2, SLOTS])
        is_top = sb("is_top", [P, 2, SLOTS, E])
        first = sb("first", [P, 2, SLOTS])
        choice = sb("choice", [P, 2, E, SLOTS])
        chosen = sb("chosen", [P, E, SLOTS])
        second = sb("second", [P, 3, SLOTS])
        w_out = sb("w_out", [P, B, C])

        upper = sb("upper", [P, P])
        none = sb("none", [P, P])
        many_i = sb("many_i", [P, MOST], I32)
        many = sb("many", [P, MOST])
        block_no_i = sb("block_no_i", [1, BLOCKS], I32)
        block_no = sb("block_no", [1, BLOCKS])
        counts = sb("counts", [P, 2, E * SLOTS])
        run_total = sb("run_total", [P, E * SLOTS])
        expert_end = sb("expert_end", [P, 1 + E])
        expert_count = sb("expert_count", [P, E])
        over = sb("over", [P, E, MOST])
        blocks_of = sb("blocks_of", [P, E])
        blocks_end = sb("blocks_end", [P, E])
        blocks_start = sb("blocks_start", [P, E])
        pad = sb("pad", [P, E])
        place = sb("place", [P, E, SLOTS])
        masked = sb("masked", [P, 2, E, SLOTS])
        row_f = sb("row_f", [P, 2, SLOTS])
        row = sb("row", [P, PAIRS, 2, SLOTS], I32)
        passed = sb("passed", [1, BLOCKS, E - 1])
        expert_f = sb("expert_f", [1, BLOCKS])
        expert_of = sb("expert_of", [1, PAIRS, BLOCKS], I32)

        rows_sb = sb("rows_sb", [P, BUFFERS, CHUNK, WIDE])
        back_row = sb("back_row", [P, BUFFERS, CHUNK], I32)
        rows_t = sb("rows_t", [P, 2, P])
        hid = sb("hid", [P, 2, F])
        hid_t = sb("hid_t", [P, 2, FC, P])
        sorted_h = [nc.dram_tensor(f"sorted_h{i}", (BLOCKS * P, WIDE), F32).ap() for i in range(PAIRS)]
        back_y = [nc.dram_tensor(f"back_y{i}", (BACK_ROWS + EMPTY_BLOCKS * P, C), F32).ap() for i in range(PAIRS)]
        h2 = sb("h2", [P, SLOTS, WIDE])
        tags = sb("tags", [P, 2, SLOTS, 2])
        tag_i = sb("tag_i", [P, 2, SLOTS], I32)
        spare_i = sb("spare_i", [P, EMPTY_BLOCKS], I32)

        ps_t = ps("ps_t", [P, J * P])
        ps_v = ps("ps_v", [P, J * P])
        ps_h = ps("ps_h", [P, 2, 512])
        ps_y = ps("ps_y", [P, 2, 512])

        weights_in, polar_in, mod_in, x_in, ident_in, experts_in = (
            sem(n) for n in ("weights_in", "polar_in", "mod_in", "x_in", "ident_in", "experts_in"))
        consts = sem("consts")
        dve_const = sem("dve_const")
        silu_exp, silu_ready = sem("silu_exp"), sem("silu_ready")
        gram_done, gram_copied, gram_t_ready = sem("gram_done"), sem("gram_copied"), sem("gram_t_ready")
        square_done, poly_ready = sem("square_done"), sem("poly_ready")
        next_done, next_copied, next_t_copied = sem("next_done"), sem("next_copied"), sem("next_t_copied")
        norm_sum, norm_total, norm_ready, w_scan_ready = (
            sem("norm_sum"), sem("norm_total"), sem("norm_ready"), sem("w_scan_ready"))
        t_full, t_free, v_full, v_free = sem("t_full"), sem("t_free"), sem("v_full"), sem("v_free")
        rows_t_full, rows_t_ready, hid_full, hid_ready = (
            sem("rows_t_full"), sem("rows_t_ready"), sem("hid_full"), sem("hid_ready"))
        hid_t_full, hid_t_ready, y_full, y_ready = (
            sem("hid_t_full"), sem("hid_t_ready"), sem("y_full"), sem("y_ready"))
        empty_ready, emptied, tagged = sem("empty_ready"), sem("emptied"), sem("tagged")
        rows_in = [sem(f"rows_in{i}") for i in range(BUFFERS)]
        rows_back = [sem(f"rows_back{i}") for i in range(BUFFERS)]
        scattered = [sem(f"scattered{b}") for b in range(B)]
        back_in = [sem(f"back_in{b}") for b in range(B)]
        centred_ready, sq_ready, var_ready, var_ln, var_exp, h_ready = (
            sem("centred_ready"), sem("sq_ready"), sem("var_ready"), sem("var_ln"), sem("var_exp"), sem("h_ready"))
        left_in = [sem("left_in0"), sem("left_in1")]
        keys_ready, pool_prod, own_prod = sem("keys_ready"), sem("pool_prod"), sem("own_prod")
        summed, terms_ready, pool_sum = sem("summed"), sem("terms_ready"), sem("pool_sum")
        shifted_ready, expo_ready, z_ready, zsq_ready = (
            sem("shifted_ready"), sem("expo_ready"), sem("z_ready"), sem("zsq_ready"))
        arg_ready, guess_ready, root_ready, scaled, own_scaled, half_ready, state_ready = (
            sem("arg_ready"), sem("guess_ready"), sem("root_ready"), sem("scaled"), sem("own_scaled"), sem("half_ready"),
            sem("state_ready"))
        w_out_ready, qv_ready, scaled2_ready, h2_ready = (
            sem("w_out_ready"), sem("qv_ready"), sem("scaled2_ready"), sem("h2_ready"))
        lead_ready, second_exp, chosen_ready, place_ready, weight_ready, back_row_ready = (
            sem("lead_ready"), sem("second_exp"), sem("chosen_ready"), sem("place_ready"), sem("weight_ready"),
            sem("back_row_ready"))
        final_ready, stored = sem("final_ready"), sem("stored")
        dve_done, act_done, pool_done = sem("dve_done"), sem("act_done"), sem("pool_done")

        T_EARLY, V_EARLY = 3, 2
        t_use, v_use = {}, {}
        for b in range(B):
            t_use["h", b], t_use["v", b] = 2 * len(t_use) + T_EARLY, 2 * len(t_use) + T_EARLY + 2
            v_use["q", b] = len(v_use) + V_EARLY
        beside = {}

        def put(position, *item):
            beside.setdefault(position, []).append(item)

        for pair in range(PAIRS):
            b0, b1 = 2 * pair, 2 * pair + 1
            at = (pair + 1) * 2 * LEVELS - 1
            put(at - 1, "qv", b0)
            put(at, "proj", b0)
            if pair < PAIRS - 1:
                put(at, "qv", b1)
                put(at + 1, "proj_out", b0)
                put(at + 1, "residual", b0)
                put(at + 1, "squares", b0)
                put(at + 1, "proj", b1)
                put(at + 1, "variance", b0)
                put(at + 2, "proj_out", b1)
                put(at + 2, "residual", b1)
                put(at + 2, "inverse_root", b0)
                put(at + 2, "squares", b1)
                put(at + 2, "modulate", b0)
                put(at + 2, "variance", b1)
                put(at + 2, "shift", b0)
                put(at + 3, "gate", b0)
                put(at + 3, "inverse_root", b1)
                put(at + 3, "modulate", b1)
                put(at + 3, "shift", b1)
                put(at + 4, "gate", b1)
                put(at + 4, "choose", pair)
                placed = at + 5
            else:
                put(at, "proj_out_early", b0)
                put(at + 1, "residual", b0)
                put(at + 1, "qv_own", b1)
                for b in (b0, b1):
                    if b == b1:
                        put(at + 2, "proj_out", b1)
                        put(at + 2, "residual", b1)
                        put(at + 2, "gate", b0)
                    position = at + 1 + b - b0
                    put(position, "squares", b)
                    put(position, "variance", b)
                    put(position, "inverse_root", b)
                    put(position, "modulate", b)
                    put(position, "shift_own", b)
                    if b == b0:
                        put(at + 1, "proj", b1)
                put(at + 3, "gate", b1)
                put(at + 3, "choose", pair)
                placed = at + 3
            put(placed, "second_exp", pair)
            put(placed, "weigh", pair)
            put(placed, "count", pair)
            put(placed, "place", pair)
            if pair < PAIRS - 1:
                starts = range(0, 2 * SLOTS, SCATTERS)
                for k, i in enumerate(starts):
                    put(placed + 1 + k, "scatter_early", pair, i, min(i + 2, 2 * SLOTS))
                    put(placed + 1 + k, "scatter", pair, i + 2, min(i + SCATTERS, 2 * SLOTS))
                load_at = placed + 1 + len(starts) + 1
            else:
                load_at = placed + 1
            for q in range(pair * CHUNKS, pair * CHUNKS + BUFFERS):
                put(load_at, "load", q)
            if pair == 0:
                steps_at = load_at
        last_stage = len(order) - 1
        position = steps_at

        def put_step(position, pair, i, here):
            put(position, "step", pair, i)
            if i >= 3:
                put(position, "back_early" if here < 2 and position <= last_stage else "back", pair, i - 3)

        here, sent, left_over = 0, 0, None
        for i in range(BLOCKS + 3):
            if position == load_at - 1:
                left_over = left_over or BLOCKS + 3 - i
                n = -(-2 * SLOTS // left_over)
                put(position, "scatter", 1, sent, min(sent + n, 2 * SLOTS))
                sent = min(sent + n, 2 * SLOTS)
            put_step(position, 0, i, here)
            here += 1
            while here >= (STEPS_BESIDE if position <= last_stage else STEPS_AFTER) and position < load_at - 1:
                position, here = position + 1, 0
        put(load_at - 1, "scatter", 1, sent, 2 * SLOTS)
        last = load_at
        for i in range(BLOCKS + 3):
            put_step(last, 1, i, i)
        for b in range(B):
            put(last + (0 if b < 2 else 1), "final", b)
        positions = max(beside) + 1

        h_users = [(("h", b), ("q", b)) for b in range(B)]
        for n in range(positions):
            if n < len(order):
                t_use[order[n]], v_use[order[n]] = 2 * len(t_use) + T_EARLY, len(v_use) + V_EARLY
            for kind, *of in beside.get(n, ()):
                if kind == "proj":
                    t_use["qv", of[0]], v_use["proj", of[0]] = 2 * len(t_use) + T_EARLY, len(v_use) + V_EARLY
                    h_users.append((("qv", of[0]), ("proj", of[0])))
                if kind == "gate":
                    t_use["h2", of[0]], v_use["gate", of[0]] = 2 * len(t_use) + T_EARLY, len(v_use) + V_EARLY
                    h_users.append((("h2", of[0]), ("gate", of[0])))
                if kind == "count":
                    v_use["count", of[0]] = len(v_use) + V_EARLY

        def run_beside(n, does):
            for kind, *of in beside.get(n, ()):
                if kind in does:
                    does[kind](*of)

        def centre_step(b):
            return 3 * b if b else 0

        def variance_step(b):
            return 3 * b + 1 if b else 1

        def scale_step(b):
            return 3 * b + 2 if b else 2

        def transpose_step(b):
            return 3 * b + 4

        LEFT_DMAS = 3

        def left_count(b, level):
            return 16 * LEFT_DMAS * sum(bb % 2 == b % 2 for bb, _ in order[:order.index((b, level)) + 1])

        def chunk_blocks(q):
            return min(CHUNK, BLOCKS - q % CHUNKS * CHUNK)

        def back_count(q):
            return 16 * sum(chunk_blocks(r) for r in range(q % BUFFERS, q + 1, BUFFERS))

        def in_chunk(pair, i):
            q = pair * CHUNKS + i // CHUNK
            return q, q % BUFFERS, i % CHUNK

        def pool_halves(n):
            return 1 if n < 2 * LEVELS - 3 or n >= len(order) - 6 else 0

        block = ctx.enter_context(nc.Block())

        @block.sync
        def _(sp):
            sp.dma_start(scan_raw[:], W_scan_raw).then_inc(polar_in, 16)
            sp.dma_start(wmod_sb, wmod).then_inc(mod_in, 16)
            for b in range(B):
                sp.dma_start(x_sb[:, b], x[b].rearrange("(p j) c -> p j c", j=J)).then_inc(x_in, 16)
            sp.dma_start(w1_sb[:], w1.rearrange("e c f -> c e f")).then_inc(experts_in, 16)
            sp.dma_start(w2_sb[:], w2.rearrange("e (k p) c -> p e k c", p=P)).then_inc(experts_in, 16)

            sp.wait_ge(empty_ready, 1)
            for pair in range(PAIRS):
                for a in range(0, BLOCKS, EMPTY_BLOCKS):
                    n = min(EMPTY_BLOCKS, BLOCKS - a)
                    sp.dma_start(sorted_h[pair].rearrange("(a p) c -> p a c", p=P)[:, a:a + n],
                                 empty[:, 0:n]).then_inc(emptied, 16)

            sp.wait_ge(ident_in, 16)
            for n, (b, level) in enumerate(order):
                d = 1 << level
                dst, src, mid = left[:, b % 2], q_sb[:, b], J // 2
                if level == 0:
                    sp.wait_ge(v_free, v_use["q", b] + 1)
                    if b >= 2:
                        sp.wait_ge(state_ready, order.index((b - 2, LEVELS - 1)) + 1)
                if d < J:
                    if level > 0:
                        sp.wait_ge(state_ready, order.index((b, level - 1)) + 1)
                    sp.dma_start(dst[:, d:J], src[:, 0:J - d]).then_inc(left_in[b % 2], 16)
                    sp.dma_start(dst[1:P, 0:d], src[0:P - 1, J - d:J]).then_inc(left_in[b % 2], 16)
                    sp.dma_start(dst[0:1, 0:d], ident[0:1, 0:d]).then_inc(left_in[b % 2], 16)
                else:
                    a = d // J
                    sp.wait_ge(half_ready, order.index((b, level - 1)) + 1)
                    sp.dma_start(dst[a:P, 0:mid], src[0:P - a, 0:mid]).then_inc(left_in[b % 2], 16)
                    sp.wait_ge(state_ready, order.index((b, level - 1)) + 1)
                    sp.dma_start(dst[a:P, mid:J], src[0:P - a, mid:J]).then_inc(left_in[b % 2], 16)
                    sp.dma_start(dst[0:a], ident[0:a]).then_inc(left_in[b % 2], 16)

            for b in range(B):
                if b % 2 == 0:
                    for q in range((b // 2 + 1) * CHUNKS - BUFFERS, (b // 2 + 1) * CHUNKS):
                        sp.wait_ge(rows_back[q % BUFFERS], back_count(q))
                for k, dst in enumerate((v_sb, q_sb)):
                    start = (b % 2 * 2 + k) * J * P
                    sp.dma_start(dst[:, b], back_y[b // 2][start:start + J * P]
                                 .rearrange("(p j) c -> p j c", j=J)).then_inc(back_in[b], 16)

            for b in range(B):
                sp.wait_ge(final_ready, b + 1)
                sp.dma_start(out[b].rearrange("(p j) c -> p j c", j=J), x_sb[:, b]).then_inc(stored, 16)
            sp.wait_ge(stored, 16 * B)

        @block.gpsimd
        def _(pool):
            nc.gpsimd.memset(eye[:], 0.0).then_inc(pool_done, 1)
            pool.wait_ge(pool_done, 1)
            nc.gpsimd.affine_select(out=eye[:], in_=eye[:], compare_op=ALU.not_equal, fill=1.0, base=0,
                                    pattern=[[-1, P]], channel_multiplier=1).then_inc(consts, 1)
            nc.gpsimd.memset(empty, 0.0).then_inc(tagged, 1)
            nc.gpsimd.iota(spare_i[:], [[P, EMPTY_BLOCKS]], base=BACK_ROWS, channel_multiplier=1).then_inc(tagged, 1)
            for k in range(2):
                nc.gpsimd.iota(tag_i[:, k], [[2 * J * P, 2], [1, J]], base=k * J * P,
                               channel_multiplier=J).then_inc(tagged, 1)
            pool.wait_ge(tagged, 4)
            nc.gpsimd.tensor_copy(empty[:, :, C], spare_i[:]).then_inc(empty_ready, 1)
            nc.gpsimd.tensor_copy(tags[:, :, :, 0], tag_i[:]).then_inc(tagged, 1)
            nc.gpsimd.memset(upper[:], 0.0).then_inc(pool_done, 1)
            pool.wait_ge(pool_done, 2)
            nc.gpsimd.affine_select(out=upper[:], in_=upper[:], compare_op=ALU.is_ge, fill=1.0, base=0,
                                    pattern=[[-1, P]], channel_multiplier=1).then_inc(consts, 1)
            nc.gpsimd.iota(many_i[:], [[P, MOST]], base=0, channel_multiplier=0).then_inc(consts, 1)
            nc.gpsimd.iota(block_no_i[:], [[1, BLOCKS]], base=0, channel_multiplier=0).then_inc(consts, 1)
            tt = nc.gpsimd.tensor_tensor

            def differences(n):
                b, level = order[n]
                if level == 0:
                    pool.wait_ge(v_free, v_use["q", b] + 1)
                else:
                    pool.wait_ge(state_ready, order.index((b, level - 1)) + 1)
                if n >= 1:
                    pool.wait_ge(own_prod, n)
                    pool.wait_ge(pool_prod, OTHERS * n)
                q4 = q_sb[:, b].rearrange("p j (l d) -> p j l d", l=LANES)
                tt(keys[:], q4[:, :, 1:LANES, :], q4[:, :, 0:1, :].to_broadcast([P, J, KEYS, HD]),
                   ALU.subtract).then_inc(keys_ready, 1)

            def products(n):
                b, level = order[n]
                s = b % 2
                pool.wait_ge(left_in[s], left_count(b, level))
                pool.wait_ge(keys_ready, n + 1)
                if n >= 1:
                    pool.wait_ge(summed, 2 * n)
                l4 = left[:, s].rearrange("p j (l d) -> p j l d", l=LANES)
                for l in range(SPLIT, LANES):
                    tt(prod[:, :, l], l4[:, :, l:l + 1, :].to_broadcast([P, J, KEYS, HD]), keys[:],
                       ALU.mult).then_inc(pool_prod, 1)

            def add_terms(n):
                s = order[n][0] % 2
                pool.wait_ge(terms_ready, n + 1)
                tt(z[:, s].rearrange("p j (l d) -> p j l d", l=LANES), terms[:, :, :, 0], terms[:, :, :, 1],
                   ALU.add).then_inc(pool_sum, 1)

            pool_scaled = [0]

            def finish(n):
                b, level = order[n]
                s = b % 2
                for half, ready in ((0, half_ready), (1, state_ready)):
                    at = slice(half * J // 2, (half + 1) * J // 2)
                    if half >= 2 - pool_halves(n):
                        pool.wait_ge(root_ready, n + 1)
                        z4 = z[:, s, at].rearrange("p j (l d) -> p j l d", l=LANES)
                        tt(z4, z4, root[:, s, at].rearrange("p j (l d) -> p j l d", d=1)
                           .to_broadcast([P, J // 2, LANES, HD]), ALU.mult).then_inc(scaled, 1)
                        pool_scaled[0] += 1
                        pool.wait_ge(scaled, pool_scaled[0])
                    else:
                        pool.wait_ge(own_scaled, n + 1)
                    tt(q_sb[:, b, at], left[:, s, at], z[:, s, at], ALU.add).then_inc(ready, 1)

            def qv(b):
                pool.wait_ge(state_ready, order.index((b, LEVELS - 1)) + 1)
                tt(q_sb[:, b], q_sb[:, b], v_sb[:, b], ALU.mult).then_inc(qv_ready, 1)

            def shift(b):
                s = b % 2
                pool.wait_ge(scaled2_ready, b + 1)
                tt(h2[:, s * J:(s + 1) * J, 0:C], v_sb[:, b], mod[:, b, SB:SB + 1, :].to_broadcast([P, J, C]),
                   ALU.add).then_inc(h2_ready, 1)

            tag_count = [5]

            def scatter(pair, start, end):
                if start == 0 < end:
                    pool.wait_ge(place_ready, pair + 1)
                    pool.wait_ge(weight_ready, pair + 1)
                    pool.wait_ge(emptied, 16 * PAIRS * 2)
                for n in range(start, end):
                    k, i = divmod(n, SLOTS)
                    b = 2 * pair + i // J
                    if i % J == 0:
                        if k == 1:
                            pool.wait_ge(scattered[b], 16 * J)
                        nc.gpsimd.tensor_copy(h2[:, i:i + J, C:], tags[:, k, i:i + J]).then_inc(tagged, 1)
                        tag_count[0] += 1
                        pool.wait_ge(tagged, tag_count[0])
                    nc.gpsimd.indirect_dma_start(
                        out=sorted_h[pair], out_offset=bass.IndirectOffsetOnAxis(ap=row[:, pair, k, i:i + 1], axis=0),
                        in_=h2[:, i, :], in_offset=None, bounds_check=BLOCKS * P - 1).then_inc(scattered[b], 16)

            def back(pair, i):
                q, buf, k = in_chunk(pair, i)
                n = chunk_blocks(q)
                if k == 0:
                    pool.wait_ge(rows_in[buf], 16 * (q // BUFFERS + 1))
                    nc.gpsimd.tensor_copy(back_row[:, buf, 0:n], rows_sb[:, buf, 0:n, C]).then_inc(back_row_ready, 1)
                    pool.wait_ge(back_row_ready, q + 1)
                pool.wait_ge(y_ready, pair * BLOCKS + i + 1)
                nc.gpsimd.indirect_dma_start(
                    out=back_y[pair], out_offset=bass.IndirectOffsetOnAxis(ap=back_row[:, buf, k:k + 1], axis=0),
                    in_=rows_sb[:, buf, k, 0:C], in_offset=None,
                    bounds_check=BACK_ROWS + EMPTY_BLOCKS * P - 1).then_inc(rows_back[buf], 16)

            differences(0)
            products(0)
            differences(1)
            for n in range(positions):
                if n < len(order):
                    add_terms(n)
                    if n + 1 < len(order):
                        products(n + 1)
                    run_beside(n, {"scatter_early": scatter, "back_early": back})
                    finish(n)
                    if n + 2 < len(order):
                        differences(n + 2)
                run_beside(n, {"scatter": scatter, "back": back, "shift": shift, "qv": qv})

        @block.scalar
        def _(act):
            act.dma_start(ct[:], c.rearrange("b c -> c b"), allow_slow_non_contiguous=True).then_inc(mod_in, 16)
            act.dma_start(w_raw[:, 0], W_up).then_inc(weights_in, 16)
            act.dma_start(w_raw[:, 1], W_v).then_inc(weights_in, 16)
            act.dma_start(w_raw[:, 2], W_proj).then_inc(weights_in, 16)
            act.dma_start(gate[:], gate_w).then_inc(weights_in, 16)
            act.dma_start(ident_row[:], identity.rearrange("(a c) -> a c", a=1)
                          .to_broadcast([P // 2, C])).then_inc(ident_in, 16)
            nc.scalar.preload_act_table_set("natural_log_exp_and_others")
            act.wait_ge(mod_in, 32)
            nc.scalar.activation(ct_e[:], ct[:], ACT.Exp, scale=-1.0).then_inc(silu_exp, 1)
            def modulation_out(b):
                area, full, free = ((ps_t, t_full, t_free), (ps_v, v_full, v_free))[b % 2]
                act.wait_ge(full, b // 2 + 1)
                nc.scalar.activation(mod[:, b].rearrange("p (a m) c -> p a (m c)", a=2),
                                     area[:].rearrange("p (a n) -> p a n", a=2)[:, :, 0:3 * C],
                                     ACT.Copy).then_inc(free, 1)

            def weights_out():
                act.wait_ge(t_full, 3)
                nc.scalar.activation(w_t[:], ps_t[:, 0:3 * P].rearrange("p (n c) -> p n c", n=3),
                                     ACT.Copy).then_inc(t_free, 1)

            def evacuate(dst, key, halves=(0, 1)):
                for half in halves:
                    at = slice(half * 512, (half + 1) * 512)
                    act.wait_ge(t_full, t_use[key] + half + 1)
                    nc.scalar.activation(dst[:, at], ps_t[:, at], ACT.Copy).then_inc(t_free, 1)

            def q_out(b):
                act.wait_ge(v_full, v_use["q", b] + 1)
                nc.scalar.activation(q_sb[:, b].rearrange("p j c -> p (j c)"), ps_v[:], ACT.Copy).then_inc(v_free, 1)

            def v_out(b):
                evacuate(v_sb[:, b].rearrange("p j c -> p (j c)"), ("v", b))

            def squares(k):
                act.wait_ge(centred_ready, k + 1)
                b = k % B
                nc.scalar.activation(q_sb[:, b], v_sb[:, b], ACT.Square, scale=float(C) ** -0.5).then_inc(sq_ready, 1)

            def inverse_root(k):
                act.wait_ge(var_ready, k + 1)
                b = k % B
                nc.scalar.activation(stat[:, b, 2], stat[:, b, 1], ACT.Ln).then_inc(var_ln, 1)
                act.wait_ge(var_ln, k + 1)
                nc.scalar.activation(stat[:, b, 3], stat[:, b, 2], ACT.Exp, scale=-0.5).then_inc(var_exp, 1)

            act.wait_ge(gram_done, 1)
            nc.scalar.activation(gram_sq[:], ps_h[:, 0, 0:P], ACT.Square, accum_out=norm_in[:]).then_inc(norm_sum, 1)
            act.wait_ge(norm_total, 2)
            nc.scalar.activation(norm_ln[:], norm_in[:], ACT.Ln).then_inc(act_done, 1)
            act.wait_ge(act_done, 1)
            nc.scalar.activation(norm[:], norm_ln[:], ACT.Exp, scale=-0.25).then_inc(norm_ready, 1)
            act.wait_ge(norm_ready, 1)
            nc.scalar.activation(polar[:, 0], scan_raw[:], ACT.Copy, scale=norm[:]).then_inc(next_copied, 1)
            act.wait_ge(gram_done, 2)
            nc.scalar.activation(polar[:, 1], ps_h[:, 0, P:2 * P], ACT.Copy, scale=norm[:]).then_inc(next_t_copied, 1)
            for k in range(POLAR_STEPS):
                act.wait_ge(next_done, k + 1)
                nc.scalar.activation(polar[:, 1], ps_y[:, 1, 0:P], ACT.Copy).then_inc(next_t_copied, 1)
                if k < 2:
                    modulation_out(2 * k)
                    modulation_out(2 * k + 1)
                elif k == 2:
                    weights_out()
                for b in range(B):
                    if k == centre_step(b):
                        squares(b)
                    if k == variance_step(b):
                        inverse_root(b)
                    if k == transpose_step(b):
                        evacuate(h_t[:], ("h", b))
                    if k == transpose_step(b) + 2:
                        q_out(b)
                    if k == transpose_step(b) + 3:
                        v_out(b)
            q_out(B - 1)
            v_out(B - 1)

            def root_guess(n):
                s = order[n][0] % 2
                act.wait_ge(arg_ready, n + 1)
                nc.scalar.activation(ln_arg[:, s], arg[:, s], ACT.Ln).then_inc(act_done, 1)
                act.wait_ge(act_done, 2 * n + 2)
                nc.scalar.activation(guess[:, s], ln_arg[:, s], ACT.Exp, scale=-0.5).then_inc(act_done, 1)
                act.wait_ge(act_done, 2 * n + 3)
                nc.scalar.activation(newton[:, s], guess[:, s], ACT.Square, scale=0.5 ** 0.5).then_inc(guess_ready, 1)

            def square_out(n):
                s = order[n][0] % 2
                act.wait_ge(z_ready, n + 1)
                nc.scalar.activation(z_sq[:], z[:, s], ACT.Square, scale=float(HD) ** -0.5).then_inc(zsq_ready, 1)

            def transposed_out(use):
                at = [key for key, _ in h_users].index(use)
                act.wait_ge(v_full, v_use[h_users[at - 1][1]] + 1)
                evacuate(h_t, use)

            def proj(b):
                transposed_out(("qv", b))

            def proj_out(b):
                act.wait_ge(v_full, v_use["proj", b] + 1)
                nc.scalar.activation(v_sb[:, b].rearrange("p j c -> p (j c)"), ps_v[:], ACT.Copy).then_inc(v_free, 1)

            def gate_out(b):
                transposed_out(("h2", b))
                act.wait_ge(v_full, v_use["gate", b] + 1)
                at = slice(b % 2 * J, (b % 2 + 1) * J)
                nc.scalar.activation(logit[:, 0, at].rearrange("p j e -> p (j e)"), ps_v[:, 0:J * E],
                                     ACT.Copy).then_inc(v_free, 1)

            def exponential(pair):
                act.wait_ge(lead_ready, pair + 1)
                nc.scalar.activation(second[:, 1], second[:, 0], ACT.Exp).then_inc(second_exp, 1)

            def count(pair):
                act.wait_ge(v_full, v_use["count", pair] + 1)
                nc.scalar.activation(counts[:].rearrange("p a n -> p (a n)"), ps_v[:, 0:2 * E * SLOTS],
                                     ACT.Copy).then_inc(v_free, 1)

            def load(q):
                pair, c = divmod(q, CHUNKS)
                if q >= BUFFERS:
                    act.wait_ge(rows_back[q % BUFFERS], back_count(q - BUFFERS))
                if c == 0:
                    for b in (2 * pair, 2 * pair + 1):
                        act.wait_ge(scattered[b], 16 * 2 * J)
                n = chunk_blocks(q)
                act.dma_start(rows_sb[:, q % BUFFERS, 0:n], sorted_h[pair][c * CHUNK * P:(c * CHUNK + n) * P]
                              .rearrange("(k p) c -> p k c", p=P)).then_inc(rows_in[q % BUFFERS], 16)

            def expert_step(pair, i):
                g = pair * BLOCKS + i
                if i < BLOCKS:
                    act.wait_ge(rows_t_full, g + 1)
                    if g >= 2:
                        act.wait_ge(hid_full, g - 1)
                    nc.scalar.activation(rows_t[:, g % 2], ps_y[:, 0, 0:P], ACT.Copy).then_inc(rows_t_ready, 1)
                if 0 <= i - 1 < BLOCKS:
                    act.wait_ge(hid_full, g)
                    if g >= 3:
                        act.wait_ge(hid_t_full, g - 2)
                    nc.scalar.activation(hid[:, (g - 1) % 2], ps_h[:, 0], ACT.Gelu).then_inc(hid_ready, 1)
                if 0 <= i - 2 < BLOCKS:
                    act.wait_ge(hid_t_full, g - 1)
                    if g >= 4:
                        act.wait_ge(y_full, g - 3)
                    nc.scalar.activation(hid_t[:, g % 2].rearrange("p f t -> p (f t)"), ps_h[:, 1],
                                         ACT.Copy).then_inc(hid_t_ready, 1)
                if 0 <= i - 3 < BLOCKS:
                    act.wait_ge(y_full, g - 2)
                    _, buf, k = in_chunk(pair, i - 3)
                    nc.scalar.activation(rows_sb[:, buf, k, 0:C], ps_y[:, 1, 0:C], ACT.Copy,
                                         scale=rows_sb[:, buf, k, C + 1:C + 2]).then_inc(y_ready, 1)
                if i % CHUNK == 1 and BUFFERS <= i // CHUNK + 1 < CHUNKS:
                    load(pair * CHUNKS + i // CHUNK + 1)

            for n in range(positions):
                if n == len(order):
                    square_out(n - 1)
                    root_guess(n - 1)
                if n < len(order):
                    b, level = order[n]
                    s = b % 2
                    if n >= 1:
                        square_out(n - 1)
                        act.wait_ge(v_full, v_use[order[n - 1]] + 1)
                    evacuate(both_t, (b, level), [0])
                    if n >= 1:
                        root_guess(n - 1)
                    evacuate(both_t, (b, level), [1])
                run_beside(n, {"proj_out": proj_out})
                if n < len(order):
                    act.wait_ge(shifted_ready, n + 1)
                    nc.scalar.activation(expo[:, s], shifted[:, s], ACT.Exp, scale=SCALE).then_inc(expo_ready, 1)
                run_beside(n, {"proj": proj, "proj_out_early": proj_out, "squares": lambda b: squares(B + b),
                               "gate": gate_out,
                               "inverse_root": lambda b: inverse_root(B + b), "second_exp": exponential,
                               "count": count, "load": load, "step": expert_step})
                if any(kind == "step" for kind, *_ in beside.get(n, ())):
                    nc.scalar.preload_act_table_set("natural_log_exp_and_others")

        @block.tensor
        def _(pe):
            def transposes(src, key, ready=None):
                pe.wait_ge(t_free, t_use[key])
                for half in range(2):
                    if ready is not None:
                        pe.wait_ge(*ready[half])
                    for j in range(half * J // 2, (half + 1) * J // 2):
                        last = nc.tensor.transpose(ps_t[:, j * P:(j + 1) * P], src[:, j], eye[:])
                    last.then_inc(t_full, 1)

            def both_transposed(b, level):
                pe.wait_ge(t_free, t_use[b, level])
                if level == 0:
                    pe.wait_ge(v_free, v_use["q", b] + 1)
                else:
                    pe.wait_ge(state_ready, order.index((b, level - 1)) + 1)
                pe.wait_ge(left_in[b % 2], left_count(b, level))
                for j in range(J):
                    nc.tensor.matmul(ps_t[:, j * P:(j + 1) * P], q_sb[:, b, j], eye[:], start=True, stop=False)
                    last = nc.tensor.matmul(ps_t[:, j * P:(j + 1) * P], left[:, b % 2, j], eye[:], start=False,
                                            stop=True)
                    if j % (J // 2) == J // 2 - 1:
                        last.then_inc(t_full, 1)

            def products(src_t, rhs, key, width, t_key):
                pe.wait_ge(v_free, v_use[key])
                for j in range(J):
                    if j % (J // 2) == 0:
                        pe.wait_ge(t_free, t_use[t_key] + j // (J // 2) + 1)
                    last = nc.tensor.matmul(ps_v[:, j * width:(j + 1) * width], src_t[:, j * P:(j + 1) * P], rhs,
                                            start=True, stop=True)
                last.then_inc(v_full, 1)

            def modulation(b):
                area, full, free = ((ps_t, t_full, t_free), (ps_v, v_full, v_free))[b % 2]
                if b == 0:
                    pe.wait_ge(silu_ready, 1)
                if b >= 2:
                    pe.wait_ge(free, 1)
                for a in range(2):
                    last = nc.tensor.matmul(area[:, a * 512:a * 512 + 3 * C], ct_silu[:, b:b + 1].to_broadcast([P, P]),
                                            wmod_sb[:, a * 3 * C:(a + 1) * 3 * C], start=True, stop=True)
                last.then_inc(full, 1)

            def weights():
                pe.wait_ge(weights_in, 64)
                pe.wait_ge(t_free, 2)
                for n in range(3):
                    last = nc.tensor.transpose(ps_t[:, n * P:(n + 1) * P], w_raw[:, n], eye[:])
                last.then_inc(t_full, 1)

            def qv_piece(b, i):
                if i == 0:
                    pe.wait_ge(v_free, v_use["q", b])
                    pe.wait_ge(t_free, t_use["h", b] + 2)
                if i < 8:
                    area, full = (ps_v, v_full) if i < 4 else (ps_t, t_full)
                    for j in (2 * (i % 4), 2 * (i % 4) + 1):
                        last = nc.tensor.matmul(area[:, j * P:(j + 1) * P], h_t[:, j * P:(j + 1) * P], w_t[:, i // 4],
                                                start=True, stop=True)
                    if i == 3 or i >= 4 and i % 2:
                        last.then_inc(full, 1)

            def beside(k, gap):
                if gap == 2 and k < 2:
                    modulation(2 * k)
                    modulation(2 * k + 1)
                if gap == 2 and k == 2:
                    weights()
                for b in range(B):
                    if gap == 2 and k == transpose_step(b):
                        pe.wait_ge(h_ready, b + 1)
                        transposes(q_sb[:, b], ("h", b))
                    i = 3 * (k - transpose_step(b) - 1) + gap
                    if 0 <= i < 9:
                        qv_piece(b, i)

            pe.wait_ge(polar_in, 16)
            nc.tensor.matmul(ps_h[:, 0, 0:P], scan_raw[:], scan_raw[:], start=True, stop=True).then_inc(gram_done, 1)
            pe.wait_ge(norm_sum, 1)
            pe.wait_ge(dve_const, 3)
            nc.tensor.matmul(ps_h[:, 1, 0:1], ones[:], norm_in[:], start=True, stop=True).then_inc(norm_total, 1)
            pe.wait_ge(consts, 1)
            nc.tensor.transpose(ps_h[:, 0, P:2 * P], scan_raw[:], eye[:]).then_inc(gram_done, 1)
            for k in range(POLAR_STEPS):
                pe.wait_ge(next_copied, k + 1)
                pe.wait_ge(next_t_copied, k + 1)
                nc.tensor.matmul(ps_h[:, 0, 0:P], polar[:, 0], polar[:, 0], start=True, stop=True).then_inc(gram_done, 1)
                beside(k, 0)
                pe.wait_ge(gram_copied, k + 1)
                nc.tensor.matmul(ps_h[:, 1, 0:P], gram[:], gram[:], start=True, stop=True).then_inc(square_done, 1)
                beside(k, 1)
                pe.wait_ge(poly_ready, k + 1)
                nc.tensor.matmul(ps_y[:, 0, 0:P], polar[:, 1], poly[:], start=True, stop=True)
                nc.tensor.matmul(ps_y[:, 1, 0:P], poly[:], polar[:, 1], start=True, stop=True).then_inc(next_done, 1)
                beside(k, 2)
            for gap in range(9):
                beside(POLAR_STEPS + gap // 3, gap % 3)

            pe.wait_ge(w_scan_ready, 1)
            def proj(b):
                pe.wait_ge(qv_ready, b + 1)
                transposes(q_sb[:, b], ("qv", b))
                pe.wait_ge(w_out_ready, 1)
                products(h_t, w_out[:, b], ("proj", b), C, ("qv", b))

            def gate_products(b):
                pe.wait_ge(h2_ready, b + 1)
                transposes(h2[:, b % 2 * J:(b % 2 + 1) * J, 0:C], ("h2", b))
                products(h_t, gate[:], ("gate", b), E, ("h2", b))

            def count(pair):
                pe.wait_ge(chosen_ready, pair + 1)
                pe.wait_ge(v_free, v_use["count", pair])
                each = chosen[:].rearrange("p e i -> p (e i)")
                nc.tensor.matmul(ps_v[:, 0:E * SLOTS], upper[:], each, start=True, stop=True)
                nc.tensor.matmul(ps_v[:, E * SLOTS:2 * E * SLOTS], ones[:], each, start=True,
                                 stop=True).then_inc(v_full, 1)

            def expert(pair, i):
                return nc.tensor.value_load(expert_of[0:1, pair, i:i + 1], min_val=0, max_val=E - 1)

            def expert_step(pair, i):
                g = pair * BLOCKS + i
                if i < BLOCKS:
                    q, buf, k = in_chunk(pair, i)
                    if k == 0:
                        pe.wait_ge(rows_in[buf], 16 * (q // BUFFERS + 1))
                    if i == 0:
                        pe.wait_ge(place_ready, pair + 1)
                        pe.wait_ge(experts_in, 32)
                    if g >= 1:
                        pe.wait_ge(rows_t_ready, g)
                    nc.tensor.transpose(ps_y[:, 0, 0:P], rows_sb[:, buf, k, 0:C], eye[:]).then_inc(rows_t_full, 1)
                if 0 <= i - 1 < BLOCKS:
                    e = expert(pair, i - 1)
                    pe.wait_ge(rows_t_ready, g)
                    if g >= 2:
                        pe.wait_ge(hid_ready, g - 1)
                    nc.tensor.matmul(ps_h[:, 0], rows_t[:, (g - 1) % 2], w1_sb[:, bass.ds(e, 1), :]
                                     .rearrange("p a f -> p (a f)"), start=True, stop=True).then_inc(hid_full, 1)
                if 0 <= i - 2 < BLOCKS:
                    pe.wait_ge(hid_ready, g - 1)
                    if g >= 3:
                        pe.wait_ge(hid_t_ready, g - 2)
                    for f in range(FC):
                        last = nc.tensor.transpose(ps_h[:, 1, f * P:(f + 1) * P], hid[:, g % 2, f * P:(f + 1) * P],
                                                   eye[:])
                    last.then_inc(hid_t_full, 1)
                if 0 <= i - 3 < BLOCKS:
                    e = expert(pair, i - 3)
                    pe.wait_ge(hid_t_ready, g - 2)
                    if g >= 4:
                        pe.wait_ge(y_ready, g - 3)
                    for f in range(FC):
                        last = nc.tensor.matmul(ps_y[:, 1, 0:C], hid_t[:, (g - 3) % 2, f],
                                                w2_sb[:, bass.ds(e, 1), f, :].rearrange("p a c -> p (a c)"),
                                                start=(f == 0), stop=(f == FC - 1))
                    last.then_inc(y_full, 1)

            for n in range(positions):
                if n < len(order):
                    b, level = order[n]
                    both_transposed(b, level)
                    products(both_t, w_scan[:], (b, level), C, (b, level))
                run_beside(n, {"proj": proj, "gate": gate_products, "count": count, "step": expert_step})

        @block.vector
        def _(dve):
            count = [0]

            def step(ins):
                ins.then_inc(dve_done, 1)
                count[0] += 1
                return count[0]

            def after(n):
                dve.wait_ge(dve_done, n)

            tt, ts, stt = nc.vector.tensor_tensor, nc.vector.tensor_scalar, nc.vector.scalar_tensor_tensor
            nc.vector.memset(ones[:], 1.0).then_inc(dve_const, 1)
            for l in range(LANES):
                last = nc.vector.memset(lane_sq[:, :, l:l + 1], float((l + 1) ** 2))
            last.then_inc(dve_const, 1)
            dve.wait_ge(consts, 1)
            after(step(ts(eye_grow[:], eye[:], GROW[0], None, ALU.mult)))
            ts(eye_polish[:], eye[:], POLISH[0], None, ALU.mult).then_inc(dve_const, 1)

            nc.vector.memset(none[:], 0.0)
            nc.vector.memset(score[:], 0.0)
            nc.vector.memset(expert_end[:], 0.0)
            for e in range(E):
                step(nc.vector.memset(early_first[:, e:e + 1], float(E - e)))
            dve.wait_ge(consts, 4)
            nc.vector.tensor_copy(many[:], many_i[:])
            after(step(nc.vector.tensor_copy(block_no[:], block_no_i[:])))

            dve.wait_ge(silu_exp, 1)
            k = step(ts(ct_e[:], ct_e[:], 1.0, None, ALU.add))
            after(k)
            k = step(nc.vector.reciprocal(ct_e[:], ct_e[:]))
            after(k)
            tt(ct_silu[:], ct[:], ct_e[:], ALU.mult).then_inc(silu_ready, 1)

            dve.wait_ge(dve_const, 3)
            dve.wait_ge(norm_total, 1)
            ts(norm_in[:], ps_h[:, 1, 0:1], 1e-18, None, ALU.max).then_inc(norm_total, 1)
            def rows(b, m):
                return mod[:, b, m:m + 1, :].to_broadcast([P, J, C])

            def per_token(a):
                return a.rearrange("p (j c) -> p j c", c=1).to_broadcast([P, J, C])

            def centre(k, b):
                n = step(nc.vector.tensor_reduce(stat[:, b, 0], x_sb[:, b], AX, ALU.add))
                after(n)
                stt(out=v_sb[:, b], in0=per_token(stat[:, b, 0]), scalar=-1.0 / C, in1=x_sb[:, b], op0=ALU.mult,
                    op1=ALU.add).then_inc(centred_ready, 1)

            def variance(k, b):
                dve.wait_ge(sq_ready, k + 1)
                n = step(nc.vector.tensor_reduce(stat[:, b, 4], q_sb[:, b], AX, ALU.add))
                after(n)
                ts(stat[:, b, 1], stat[:, b, 4], 1e-5, None, ALU.add).then_inc(var_ready, 1)

            def modulate(k, b, scale_row, shift_row):
                dve.wait_ge(var_exp, k + 1)
                st = stat[:, b]
                n = step(tt(st[:, 5], st[:, 3], st[:, 3], ALU.mult))
                after(n)
                n = step(stt(out=st[:, 6], in0=st[:, 5], scalar=-0.5, in1=st[:, 1], op0=ALU.mult, op1=ALU.mult))
                after(n)
                n = step(stt(out=st[:, 7], in0=st[:, 6], scalar=1.5, in1=st[:, 3], op0=ALU.add, op1=ALU.mult))
                after(n)
                n = step(tt(v_sb[:, b], v_sb[:, b], per_token(st[:, 7]), ALU.mult))
                after(n)
                n = tt(v_sb[:, b], v_sb[:, b], rows(b, scale_row), ALU.mult)
                if shift_row is None:
                    n.then_inc(scaled2_ready, 1)
                else:
                    n = step(n)
                if shift_row is not None:
                    after(n)
                    tt(q_sb[:, b], v_sb[:, b], rows(b, shift_row), ALU.add).then_inc(h_ready, 1)

            def scale_rows():
                for m in (CA, CB):
                    n = step(ts(mod[:, :, m], mod[:, :, m], 1.0, None, ALU.add))
                after(n)

            def gate_rows():
                for m in (GA, GB):
                    n = step(ts(sign, mod[:, :, m], 0.0, 2.0, ALU.is_ge, ALU.mult))
                    n = step(stt(out=size, in0=mod[:, :, m], scalar=-1.0, in1=mod[:, :, m], op0=ALU.mult, op1=ALU.max))
                    after(n)
                    n = step(ts(size, size, 0.25, None, ALU.max))
                    after(n)
                    n = step(stt(out=mod[:, :, m], in0=sign, scalar=-1.0, in1=size, op0=ALU.add, op1=ALU.mult))
                    after(n)

            for k in range(POLAR_STEPS):
                grow = k < GROW_STEPS
                (_, cb, cc), eye_a = (GROW, eye_grow) if grow else (POLISH, eye_polish)
                dve.wait_ge(gram_done, k + 3)
                nc.vector.tensor_copy(gram[:], ps_h[:, 0, 0:P]).then_inc(gram_copied, 1)
                stt(out=gram_t[:], in0=ps_h[:, 0, 0:P], scalar=cb, in1=eye_a[:], op0=ALU.mult,
                    op1=ALU.add).then_inc(gram_t_ready, 1)
                dve.wait_ge(square_done, k + 1)
                dve.wait_ge(gram_t_ready, k + 1)
                stt(out=poly[:], in0=ps_h[:, 1, 0:P], scalar=cc, in1=gram_t[:], op0=ALU.mult,
                    op1=ALU.add).then_inc(poly_ready, 1)
                dve.wait_ge(next_done, k + 1)
                nc.vector.tensor_copy(polar[:, 0], ps_y[:, 0, 0:P]).then_inc(next_copied, 1)
                if k == 2:
                    dve.wait_ge(t_free, 2)
                    dve.wait_ge(v_free, 2)
                    scale_rows()
                for b in range(B):
                    if k == centre_step(b):
                        dve.wait_ge(x_in, 16 * B)
                        centre(b, b)
                    if k == variance_step(b):
                        variance(b, b)
                    if k == scale_step(b):
                        modulate(b, b, CA, SA)
            dve.wait_ge(next_copied, GROW_STEPS + POLISH_STEPS + 1)
            nc.vector.tensor_copy(w_scan[:, 0:HD], polar[:, 0, 0:HD])
            tt(w_scan[:, HD:].rearrange("p (m d) -> p m d", d=HD), polar[:, 0, HD:].rearrange("p (m d) -> p m d", d=HD),
               polar[:, 0, 0:HD].rearrange("p (m d) -> p m d", m=1).to_broadcast([P, KEYS, HD]),
               ALU.subtract).then_inc(w_scan_ready, 1)

            gate_rows()
            dve.wait_ge(t_free, 3)
            tt(w_out[:], mod[:, :, GA], w_t[:, 2:3].to_broadcast([P, B, C]), ALU.mult).then_inc(w_out_ready, 1)
            dve.wait_ge(emptied, 16 * PAIRS * 2)

            def scores(n):
                b, level = order[n]
                s = b % 2
                dve.wait_ge(keys_ready, n + 1)
                dve.wait_ge(left_in[s], left_count(b, level))
                l4 = left[:, s].rearrange("p j (l d) -> p j l d", l=LANES)
                for l in range(SPLIT):
                    last = tt(prod[:, :, l], l4[:, :, l:l + 1, :].to_broadcast([P, J, KEYS, HD]), keys[:], ALU.mult)
                last.then_inc(own_prod, 1)

            def join(n):
                s = order[n][0] % 2
                dve.wait_ge(pool_sum, n + 1)
                dve.wait_ge(v_free, v_use[order[n]] + 1)
                z4 = z[:, s].rearrange("p j (l d) -> p j l d", l=LANES)
                tt(z4, z4, terms[:, :, :, 2], ALU.add).then_inc(z_ready, 1)

            def sum_products(n, own):
                s = order[n][0] % 2
                if own:
                    dve.wait_ge(own_prod, n + 1)
                dve.wait_ge(pool_prod, OTHERS * n + (1 if own else OTHERS))
                lanes = slice(0, SPLIT + 1) if own else slice(SPLIT + 1, LANES)
                nc.vector.tensor_reduce(score[:, s, :, lanes, 1:], prod[:, :, lanes], AX, ALU.add).then_inc(summed, 1)

            def mean_square(n):
                o = order[n][0] % 2
                dve.wait_ge(zsq_ready, n + 1)
                return step(nc.vector.tensor_reduce(ms[:, o], z_sq[:].rearrange("p j (l d) -> p j l d", l=LANES),
                                                    AX, ALU.add))

            def root_argument(n, k):
                o = order[n][0] % 2
                after(k)
                stt(out=arg[:, o], in0=ms[:, o], scalar=1e-8, in1=lane_sq[:], op0=ALU.add,
                    op1=ALU.mult).then_inc(arg_ready, 1)

            def soften(n):
                s = order[n][0] % 2
                dve.wait_ge(summed, 2 * n + 2)
                k = step(nc.vector.tensor_reduce(high[:, s], score[:, s], AX, ALU.max))
                after(k)
                tt(shifted[:, s], score[:, s], high[:, s].rearrange("p j (l m) -> p j l m", m=1)
                   .to_broadcast([P, J, LANES, LANES]), ALU.subtract).then_inc(shifted_ready, 1)

            def inverse_of_root(n):
                s = order[n][0] % 2
                dve.wait_ge(guess_ready, n + 1)
                k = step(stt(out=newton[:, s], in0=newton[:, s], scalar=-1.0, in1=arg[:, s], op0=ALU.mult, op1=ALU.mult))
                after(k)
                stt(out=root[:, s], in0=newton[:, s], scalar=1.5, in1=guess[:, s], op0=ALU.add,
                    op1=ALU.mult).then_inc(root_ready, 1)

            def scale(n):
                s = order[n][0] % 2
                slots = (2 - pool_halves(n)) * J // 2
                dve.wait_ge(root_ready, n + 1)
                z4 = z[:, s, 0:slots].rearrange("p j (l d) -> p j l d", l=LANES)
                tt(z4, z4, root[:, s, 0:slots].rearrange("p j (l d) -> p j l d", d=1)
                   .to_broadcast([P, slots, LANES, HD]), ALU.mult).then_inc(own_scaled, 1)

            def mix(n):
                b, level = order[n]
                s = b % 2
                dve.wait_ge(expo_ready, n + 1)
                k = step(nc.vector.tensor_reduce(total[:, s], expo[:, s], AX, ALU.add))
                after(k)
                k = step(nc.vector.reciprocal(recip[:, s], total[:, s]))
                after(k)
                k = step(tt(att[:, s], expo[:, s, :, :, 1:], recip[:, s].rearrange("p j (l m) -> p j l m", m=1)
                            .to_broadcast([P, J, LANES, KEYS]), ALU.mult))
                after(k)
                dve.wait_ge(v_full, v_use[b, level] + 1)
                v4 = ps_v[:].rearrange("p (j m d) -> p j m d", m=LANES, d=HD)
                for m in range(KEYS):
                    last = tt(terms[:, :, :, m], att[:, s, :, :, m:m + 1].to_broadcast([P, J, LANES, HD]),
                              v4[:, :, 1 + m:2 + m].to_broadcast([P, J, LANES, HD]), ALU.mult)
                    if m == 1:
                        last.then_inc(terms_ready, 1)
                after(step(last))
                tt(terms[:, :, :, 2], terms[:, :, :, 2], v4[:, :, 0:1].to_broadcast([P, J, LANES, HD]),
                   ALU.add).then_inc(v_free, 1)

            def qv(b):
                dve.wait_ge(state_ready, order.index((b, LEVELS - 1)) + 1)
                tt(q_sb[:, b], q_sb[:, b], v_sb[:, b], ALU.mult).then_inc(qv_ready, 1)

            def shift(b):
                s = b % 2
                dve.wait_ge(scaled2_ready, b + 1)
                dve.wait_ge(scattered[b - 2], 16 * 2 * J)
                tt(h2[:, s * J:(s + 1) * J, 0:C], v_sb[:, b], rows(b, SB), ALU.add).then_inc(h2_ready, 1)

            def residual(b):
                dve.wait_ge(v_free, v_use["proj", b] + 1)
                k = step(tt(x_sb[:, b], x_sb[:, b], v_sb[:, b], ALU.add))
                after(k)
                centre(B + b, b)

            def choose(pair):
                dve.wait_ge(v_free, v_use["gate", 2 * pair + 1] + 1)
                for r in range(2):
                    lg = logit[:, r]
                    k = step(nc.vector.tensor_reduce(top[:, r], lg, AX, ALU.max))
                    after(k)
                    k = step(tt(is_top[:, r], lg, top[:, r].rearrange("p (i e) -> p i e", e=1)
                                .to_broadcast([P, SLOTS, E]), ALU.is_equal))
                    if r == 1:
                        tt(second[:, 0], top[:, 1], top[:, 0], ALU.subtract).then_inc(lead_ready, 1)
                    after(k)
                    k = step(tt(is_top[:, r], is_top[:, r], early_first[:].rearrange("p (i e) -> p i e", i=1)
                                .to_broadcast([P, SLOTS, E]), ALU.mult))
                    after(k)
                    k = step(nc.vector.tensor_reduce(first[:, r], is_top[:, r], AX, ALU.max))
                    after(k)
                    mask = choice[:, r].rearrange("p e i -> p i e")
                    k = step(tt(mask, is_top[:, r], first[:, r].rearrange("p (i e) -> p i e", e=1)
                                .to_broadcast([P, SLOTS, E]), ALU.is_equal))
                    after(k)
                    if r == 0:
                        k = step(stt(out=logit[:, 1], in0=mask, scalar=-3e38, in1=lg, op0=ALU.mult, op1=ALU.add))
                        after(k)
                tt(chosen[:], choice[:, 0], choice[:, 1], ALU.add).then_inc(chosen_ready, 1)

            def weigh(pair):
                dve.wait_ge(second_exp, pair + 1)
                k = step(ts(second[:, 2], second[:, 1], 1.0, None, ALU.add))
                after(k)
                k = step(nc.vector.reciprocal(tags[:, 0, :, 1], second[:, 2]))
                after(k)
                tt(tags[:, 1, :, 1], second[:, 1], tags[:, 0, :, 1], ALU.mult).then_inc(weight_ready, 1)

            def place_rows(pair):
                dve.wait_ge(v_free, v_use["count", pair] + 1)
                k = step(nc.vector.tensor_tensor_scan(run_total[:], counts[:, 1], none[:, 0:E * SLOTS], 0.0, ALU.add,
                                                      ALU.add))
                after(k)
                by_slot = run_total[:].rearrange("p (e i) -> p e i", e=E)
                k = step(nc.vector.tensor_copy(expert_end[:, 1:], by_slot[:, :, SLOTS - 1]))
                flat = place[:].rearrange("p e i -> p (e i)")
                m = step(tt(flat, run_total[:], counts[:, 1], ALU.subtract))
                after(k)
                k = step(tt(expert_count[:], expert_end[:, 1:], expert_end[:, 0:E], ALU.subtract))
                after(m)
                step(tt(flat, flat, counts[:, 0], ALU.add))
                after(k)
                k = step(tt(over[:], expert_count[:].rearrange("p (e n) -> p e n", n=1).to_broadcast([P, E, MOST]),
                            many[:].rearrange("p (e n) -> p e n", e=1).to_broadcast([P, E, MOST]), ALU.is_gt))
                after(k)
                k = step(nc.vector.tensor_reduce(blocks_of[:], over[:], AX, ALU.add))
                after(k)
                k = step(nc.vector.tensor_tensor_scan(blocks_end[:], blocks_of[:], none[:, 0:E], 0.0, ALU.add, ALU.add))
                after(k)
                k = step(tt(blocks_start[:], blocks_end[:], blocks_of[:], ALU.subtract))
                m = step(tt(passed[:], block_no[:].rearrange("p (n e) -> p n e", e=1).to_broadcast([1, BLOCKS, E - 1]),
                            blocks_end[0:1, 0:E - 1].rearrange("p (n e) -> p n e", n=1)
                            .to_broadcast([1, BLOCKS, E - 1]), ALU.is_ge))
                after(k)
                k = step(stt(out=pad[:], in0=blocks_start[:], scalar=float(P), in1=expert_end[:, 0:E], op0=ALU.mult,
                             op1=ALU.subtract))
                after(m)
                m = step(nc.vector.tensor_reduce(expert_f[:], passed[:], AX, ALU.add))
                after(k)
                k = step(tt(place[:], place[:], pad[:].rearrange("p (e i) -> p e i", i=1)
                            .to_broadcast([P, E, SLOTS]), ALU.add))
                after(m)
                step(nc.vector.tensor_copy(expert_of[:, pair], expert_f[:]))
                after(k)
                k = step(tt(masked[:], choice[:], place[:].rearrange("p (a e) i -> p a e i", a=1)
                            .to_broadcast([P, 2, E, SLOTS]), ALU.mult))
                after(k)
                k = step(nc.vector.tensor_reduce(row_f[:], masked[:].rearrange("p a e i -> p a i e"), AX, ALU.add))
                after(k)
                nc.vector.tensor_copy(row[:, pair], row_f[:]).then_inc(place_ready, 1)

            def final(b):
                dve.wait_ge(back_in[b], 16 * 2)
                k = step(tt(v_sb[:, b], v_sb[:, b], q_sb[:, b], ALU.add))
                after(k)
                k = step(tt(v_sb[:, b], v_sb[:, b], rows(b, GB), ALU.mult))
                after(k)
                tt(x_sb[:, b], v_sb[:, b], x_sb[:, b], ALU.add).then_inc(final_ready, 1)

            for n in range(positions):
                if n < len(order):
                    scores(n)
                if 1 <= n <= len(order):
                    k = mean_square(n - 1)
                    root_argument(n - 1, k)
                if n < len(order):
                    sum_products(n, own=True)
                if 1 <= n <= len(order):
                    inverse_of_root(n - 1)
                    scale(n - 1)
                run_beside(n, {"residual": residual})
                if n < len(order):
                    sum_products(n, own=False)
                    soften(n)
                    mix(n)
                    join(n)
                run_beside(n, {"qv_own": qv, "shift_own": shift, "variance": lambda b: variance(B + b, b),
                               "modulate": lambda b: modulate(B + b, b, CB, None), "choose": choose,
                               "weigh": weigh, "place": place_rows, "final": final})


_INS = ['L0_attn_x', 'L0_attn_W_up', 'L0_attn_W_v', 'L0_attn_W_proj', 'L0_attn_identity', 'L0_attn_W_scan_raw',
        'L0_ffn_gate_w', 'L0_ffn_w1', 'L0_ffn_w2', 'L0_c', 'L0_wmod']
_OUTS = [((4, 1024, 128), 'float32')]


def kernel(**inputs):
    import numpy as _np
    import concourse.bacc as _bacc
    from concourse import mybir as _mybir
    from concourse.bass_utils import run_bass_kernel_spmd as _run

    nc = _bacc.Bacc("TRN2", target_bir_lowering=False, num_devices=1)
    arrays, args = {}, []
    for name in _INS:
        a = _np.ascontiguousarray(inputs[name])
        arrays[f"in_{name}_dram"] = a
        args.append(nc.dram_tensor(f"in_{name}_dram", a.shape, _mybir.dt.from_np(a.dtype), kind="ExternalInput").ap())
    for i, (shape, dtype) in enumerate(_OUTS):
        dt = _mybir.dt.from_np(_np.dtype(dtype))
        args.append(nc.dram_tensor(f"out_{i}_dram", shape, dt, kind="ExternalOutput").ap())
    adaln_block(nc, *args)
    r = _run(nc, [arrays], core_ids=[0])
    got = tuple(r.results[0][f"out_{i}_dram"] for i in range(len(_OUTS)))
    return got[0]
```
